# Optimizing a Trainium2 kernel written in Bass

```python
import numpy as np
import jax
import jax.numpy as jnp

def _softmax(x, axis=-1):
    return jax.nn.softmax(x, axis=axis)

def _gelu(x):
    return jax.nn.gelu(x, approximate=True)

def _silu(x):
    return jax.nn.silu(x)

def _sigmoid(x):
    return jax.nn.sigmoid(x)

def _layernorm(x, axis=-1, eps=1e-05):
    m = jnp.mean(x, axis=axis, keepdims=True)
    v = jnp.var(x, axis=axis, keepdims=True)
    return (x - m) / jnp.sqrt(v + eps)

def _scatter_add(tgt, idx, src, axis=0):
    return tgt.at[idx].add(src)

def _segment_sum(src, seg, n):
    return jax.ops.segment_sum(src, seg, n)
kernel_name = 'mk_vit_tower_d2_tok_img512_r4_b5b7ae'

def setup_inputs(seed: int=0):
    np.random.seed(seed)
    _w = jnp.asarray

    def _rec_inputs():
        import jax
        import jax.numpy as jnp
        _rk = jax.random.key(seed)
        x = -0.000147625 + 0.999875 * jax.random.normal(jax.random.fold_in(_rk, 1), (128, 3, 224, 224), jnp.float32)
        return x
    x = _rec_inputs()

    def _L0_tok_setup():
        import jax, jax.numpy as jnp
        import numpy as np
        N_PATCHES = 8
        PATCH = 28
        C = 3
        IN_D = C * PATCH * PATCH
        HID = 128
        SEQ = N_PATCHES * N_PATCHES + 1

        def _positional_embedding(seq_len, dim):
            i = np.arange(seq_len)[:, None].astype(np.float32)
            j = np.arange(dim)[None, :].astype(np.float32)
            ang = i / np.power(100000.0, j / dim)
            pe = np.where(j % 2 == 0, np.sin(ang), np.cos(ang))
            return jnp.asarray(pe, dtype=jnp.float32)
        key = jax.random.key(seed)
        k1, k2, k3, k4 = jax.random.split(key, 4)
        B = 64
        X = jax.random.normal(k1, (B, C, 224, 224), dtype=jnp.float32)
        bound = 1.0 / np.sqrt(IN_D)
        W = jax.random.uniform(k2, (HID, IN_D), minval=-bound, maxval=bound, dtype=jnp.float32)
        b = jax.random.uniform(k3, (HID,), minval=-bound, maxval=bound, dtype=jnp.float32)
        class_token = jax.random.uniform(k4, (1, HID), dtype=jnp.float32)
        pos_embed = _positional_embedding(SEQ, HID)
        return {'X': X, 'W': W, 'b': b, 'class_token': class_token, 'pos_embed': pos_embed}
    _L0_tok_all = _L0_tok_setup()
    _L0_tok_in = {k: v for k, v in _L0_tok_all.items() if k in ('W', 'b', 'class_token', 'pos_embed')}
    del _L0_tok_all

    def _L0_attn_setup():
        import jax, jax.numpy as jnp
        import numpy as np
        B, T, D, K, V = (4, 1024, 128, 128, 128)
        key = jax.random.key(seed)
        ks = jax.random.split(key, 7)
        w = lambda k, shp: jax.random.normal(k, shp, dtype=jnp.float32) * 0.02
        return {'minibatch': jax.random.normal(ks[0], (B, T, D), dtype=jnp.float32), 'Wk': w(ks[1], (D, K)), 'bk': jnp.zeros((K,), jnp.float32), 'Wq': w(ks[2], (D, K)), 'bq': jnp.zeros((K,), jnp.float32), 'Wv': w(ks[3], (D, V)), 'bv': jnp.zeros((V,), jnp.float32)}
    _L0_attn_all = _L0_attn_setup()
    _L0_attn_in = {k: v for k, v in _L0_attn_all.items() if k in ('Wk', 'bk', 'Wq', 'bq', 'Wv', 'bv')}
    del _L0_attn_all

    def _L0_ffn_setup():
        import jax, jax.numpy as jnp
        import numpy as np
        TOP_K = 2
        key = jax.random.key(seed)
        k1, k2, k3, k4 = jax.random.split(key, 4)
        B, S, d = (4, 512, 128)
        E, H = (32, 128)
        x = jax.random.normal(k1, (B, S, d), dtype=jnp.float32)
        expert_sel = jax.random.normal(k2, (E, d), dtype=jnp.float32) / np.sqrt(d).astype(np.float32)
        keys = jax.random.normal(k3, (E, d, H), dtype=jnp.float32) / np.sqrt(d).astype(np.float32)
        values = jax.random.normal(k4, (E, H, d), dtype=jnp.float32) / np.sqrt(E * H).astype(np.float32)
        return {'x': x, 'expert_sel': expert_sel, 'keys': keys, 'values': values}
    _L0_ffn_all = _L0_ffn_setup()
    _L0_ffn_in = {k: v for k, v in _L0_ffn_all.items() if k in ('expert_sel', 'keys', 'values')}
    del _L0_ffn_all

    def _L1_attn_setup():
        import jax, jax.numpy as jnp
        import numpy as np
        B, T, D = (8, 512, 128)
        key = jax.random.key(seed)
        k1, _ = jax.random.split(key)
        h = jax.random.normal(k1, (B, T, D), dtype=jnp.float32)
        k = jnp.ones((), dtype=jnp.float32)
        return {'h': h, 'k': k}
    _L1_attn_all = _L1_attn_setup()
    _L1_attn_in = {k: v for k, v in _L1_attn_all.items() if k in ('k',)}
    del _L1_attn_all

    def _L1_ffn_setup():
        import jax, jax.numpy as jnp
        import numpy as np
        from jax import lax
        N_EXPERTS = 16
        TOP_K = 2
        D_MODEL = 128
        D_FF = 512
        key = jax.random.key(seed)
        ks = jax.random.split(key, 7)
        s_in = 1.0 / np.sqrt(D_MODEL)
        s_ff = 1.0 / np.sqrt(D_FF)
        x = jax.random.normal(ks[0], (2, 512, D_MODEL), dtype=jnp.float32)
        router_w = jax.random.uniform(ks[1], (N_EXPERTS, D_MODEL), jnp.float32, -s_in, s_in)
        router_b = jax.random.uniform(ks[2], (N_EXPERTS,), jnp.float32, -s_in, s_in)
        w1 = jax.random.uniform(ks[3], (N_EXPERTS, D_FF, D_MODEL), jnp.float32, -s_in, s_in)
        b1 = jax.random.uniform(ks[4], (N_EXPERTS, D_FF), jnp.float32, -s_in, s_in)
        w2 = jax.random.uniform(ks[5], (N_EXPERTS, D_MODEL, D_FF), jnp.float32, -s_ff, s_ff)
        b2 = jax.random.uniform(ks[6], (N_EXPERTS, D_MODEL), jnp.float32, -s_ff, s_ff)
        return {'x': x, 'router_w': router_w, 'router_b': router_b, 'w1': w1, 'b1': b1, 'w2': w2, 'b2': b2}
    _L1_ffn_all = _L1_ffn_setup()
    _L1_ffn_in = {k: v for k, v in _L1_ffn_all.items() if k in ('router_w', 'router_b', 'w1', 'b1', 'w2', 'b2')}
    del _L1_ffn_all
    return {'x': x, 'L0_tok_W': _L0_tok_in['W'], 'L0_tok_b': _L0_tok_in['b'], 'L0_tok_class_token': _L0_tok_in['class_token'], 'L0_tok_pos_embed': _L0_tok_in['pos_embed'], 'L0_attn_Wk': _L0_attn_in['Wk'], 'L0_attn_bk': _L0_attn_in['bk'], 'L0_attn_Wq': _L0_attn_in['Wq'], 'L0_attn_bq': _L0_attn_in['bq'], 'L0_attn_Wv': _L0_attn_in['Wv'], 'L0_attn_bv': _L0_attn_in['bv'], 'L0_ffn_expert_sel': _L0_ffn_in['expert_sel'], 'L0_ffn_keys': _L0_ffn_in['keys'], 'L0_ffn_values': _L0_ffn_in['values'], 'L1_attn_k': _L1_attn_in['k'], 'L1_ffn_router_w': _L1_ffn_in['router_w'], 'L1_ffn_router_b': _L1_ffn_in['router_b'], 'L1_ffn_w1': _L1_ffn_in['w1'], 'L1_ffn_b1': _L1_ffn_in['b1'], 'L1_ffn_w2': _L1_ffn_in['w2'], 'L1_ffn_b2': _L1_ffn_in['b2']}

def reference(x, L0_tok_W, L0_tok_b, L0_tok_class_token, L0_tok_pos_embed, L0_attn_Wk, L0_attn_bk, L0_attn_Wq, L0_attn_bq, L0_attn_Wv, L0_attn_bv, L0_ffn_expert_sel, L0_ffn_keys, L0_ffn_values, L1_attn_k, L1_ffn_router_w, L1_ffn_router_b, L1_ffn_w1, L1_ffn_b1, L1_ffn_w2, L1_ffn_b2):
    import jax
    import jax.numpy as jnp

    def _L0_tok_ref(X, W, b, class_token, pos_embed):
        import jax, jax.numpy as jnp
        import numpy as np
        N_PATCHES = 8
        PATCH = 28
        C = 3
        IN_D = C * PATCH * PATCH
        HID = 128
        SEQ = N_PATCHES * N_PATCHES + 1

        def _positional_embedding(seq_len, dim):
            i = np.arange(seq_len)[:, None].astype(np.float32)
            j = np.arange(dim)[None, :].astype(np.float32)
            ang = i / np.power(100000.0, j / dim)
            pe = np.where(j % 2 == 0, np.sin(ang), np.cos(ang))
            return jnp.asarray(pe, dtype=jnp.float32)
        B = X.shape[0]
        patches = X.reshape(B, C, N_PATCHES, PATCH, N_PATCHES, PATCH)
        patches = patches.transpose(0, 2, 4, 1, 3, 5).reshape(B, N_PATCHES * N_PATCHES, IN_D)
        tokens = jnp.einsum('bpi,hi->bph', patches, W) + b
        cls = jnp.broadcast_to(class_token[None, :, :], (B, 1, HID))
        tokens = jnp.concatenate([cls, tokens], axis=1)
        return tokens * pos_embed[None, :, :]

    def _L0_attn_ref(minibatch, Wk, bk, Wq, bq, Wv, bv):
        import jax, jax.numpy as jnp
        import numpy as np
        B, T, D, K, V = (4, 1024, 128, 128, 128)
        keys = minibatch @ Wk + bk
        queries = minibatch @ Wq + bq
        values = minibatch @ Wv + bv
        logits = jnp.einsum('btk,bsk->bts', queries, keys)
        t = logits.shape[1]
        mask = jnp.triu(jnp.ones((t, t), dtype=bool), k=1)
        logits = jnp.where(mask[None, :, :], -jnp.inf, logits)
        sqrt_k = jnp.asarray(np.sqrt(K), dtype=logits.dtype)
        probs = jax.nn.softmax(logits, axis=1) / sqrt_k
        read = jnp.einsum('bts,bsv->btv', probs, values)
        return minibatch + read

    def _L0_ffn_ref(x, expert_sel, keys, values):
        import jax, jax.numpy as jnp
        import numpy as np
        TOP_K = 2
        B, S, d = x.shape
        E = keys.shape[0]
        xt = x.reshape(-1, d)
        T = xt.shape[0]
        sel = jax.nn.sigmoid(xt @ expert_sel.T)
        sel_val, sel_idx = jax.lax.top_k(sel, TOP_K)
        w = jnp.zeros((T, E), dtype=xt.dtype).at[jnp.arange(T)[:, None], sel_idx].add(sel_val)
        h = jax.nn.relu(jnp.einsum('td,edh->teh', xt, keys))
        out = jnp.einsum('teh,te,ehv->tv', h, w, values)
        return out.reshape(B, S, -1)

    def _L1_attn_ref(h, k):
        import jax, jax.numpy as jnp
        import numpy as np
        B, T, D = (8, 512, 128)
        Tn = h.shape[1]
        h_cum = jnp.cumsum(h, axis=1)
        h_prev = jnp.pad(h[:, :-1, :], ((0, 0), (1, 0), (0, 0)))
        delta = h_cum - h_prev
        delta_mag = jnp.linalg.norm(delta, axis=-1)
        t = jnp.arange(Tn)[:, None]
        j = jnp.arange(Tn)[None, :]
        dist = jnp.abs(t - j).astype(jnp.float32)
        decay = jnp.exp(-jax.nn.softplus(k) * dist) * (j <= t)
        context = jnp.einsum('ij,bjd->bid', decay, h)
        return jnp.abs(delta_mag[..., None] * context)

    def _L1_ffn_ref(x, router_w, router_b, w1, b1, w2, b2):
        import jax, jax.numpy as jnp
        import numpy as np
        from jax import lax
        N_EXPERTS = 16
        TOP_K = 2
        D_MODEL = 128
        D_FF = 512
        B, S, D = x.shape
        xt = x.reshape(-1, D)
        logits = xt @ router_w.T + router_b
        probs = jax.nn.softmax(logits, axis=-1)
        topk_p, topk_i = lax.top_k(probs, TOP_K)
        onehot = jax.nn.one_hot(topk_i, N_EXPERTS, dtype=probs.dtype)
        gates = jnp.sum(onehot * topk_p[..., None], axis=1)

        def expert_step(acc, packed):
            w1e, b1e, w2e, b2e, ge = packed
            h = jax.nn.gelu(xt @ w1e.T + b1e, approximate=False)
            y = h @ w2e.T + b2e
            return (acc + y * ge[:, None], None)
        out, _ = lax.scan(expert_step, jnp.zeros_like(xt), (w1, b1, w2, b2, gates.T))
        return out.reshape(B, S, D)
    h = _L0_tok_ref(x, L0_tok_W, L0_tok_b, L0_tok_class_token, L0_tok_pos_embed)
    h = h + _L0_attn_ref(_layernorm(h, axis=-1), L0_attn_Wk, L0_attn_bk, L0_attn_Wq, L0_attn_bq, L0_attn_Wv, L0_attn_bv)
    h = h + _L0_ffn_ref(_layernorm(h, axis=-1), L0_ffn_expert_sel, L0_ffn_keys, L0_ffn_values)
    h = h + _L1_attn_ref(_layernorm(h, axis=-1), L1_attn_k)
    h = h + _L1_ffn_ref(_layernorm(h, axis=-1), L1_ffn_router_w, L1_ffn_router_b, L1_ffn_w1, L1_ffn_b1, L1_ffn_w2, L1_ffn_b2)
    return h

_drawn_inputs = setup_inputs


def setup_inputs(seed=0):
    import zlib

    import numpy as np

    out = dict(_drawn_inputs(seed))
    spreads = {'L0_attn_bk': (0.0, 0.8), 'L0_attn_bq': (0.0, 2.0), 'L0_attn_bv': (0.0, 0.438)}
    factors = {'L0_tok_class_token': 3.6,
     'L0_attn_Wk': 8.0,
     'L0_attn_Wq': 7.042,
     'L0_attn_Wv': 5.239,
     'L1_ffn_router_w': 8.0,
     'L1_ffn_router_b': 8.0,
     'L1_ffn_w1': 8.0,
     'L1_ffn_b1': 29.501,
     'L1_ffn_w2': 8.0,
     'L1_ffn_b2': 195.012}
    for name, (base, spread) in spreads.items():
        noise = np.random.default_rng([zlib.crc32(name.encode()), seed]).standard_normal(out[name].shape)
        drawn = base * np.exp(spread * noise) if base else spread * noise
        out[name] = jnp.asarray(drawn.astype(out[name].dtype))
    for name, factor in factors.items():
        out[name] = (out[name] * factor).astype(out[name].dtype)
    return out
```

```python
from contextlib import ExitStack

import concourse.bass as bass
from concourse import mybir

F32 = mybir.dt.float32
BF16 = mybir.dt.bfloat16
U32 = mybir.dt.uint32
I32 = mybir.dt.int32
ALU = mybir.AluOpType
ACT = mybir.ActivationFunctionType
X = mybir.AxisListType.X

IMAGES, SEQ, D = 128, 65, 128
PATCHES = SEQ - 1
TOKENS = IMAGES * SEQ
GROUPS = 16
GI = IMAGES // GROUPS
GT = GI * SEQ
GP = GI * PATCHES
TILES = 5
ROWS = GT // TILES
HALF = GT // 2
TOP = 2
IN_D = 3 * 28 * 28
KT = IN_D // 128
KREST = IN_D - KT * 128
CHUNKS = 3
KC = KT // CHUNKS
BANK = 512
EPS = 1e-5
MASKED = -1e30
ROW = D + 4
PLACE, GATE = D, D + 1
NOWHERE = TOKENS * TOP
NB = 8


class Layer:

    def __init__(self, turn, name, experts, hidden, block, unroll=NB):
        self.turn = turn
        self.name, self.E, self.FC, self.block = name, experts, hidden // 128, block
        self.Q = block // 128
        self.shift = block.bit_length() - 1
        self.room = TOKENS + block
        most = (TOKENS * TOP + experts * (block - 1)) // block
        self.unroll = unroll
        self.blocks = -(-most // unroll) * unroll
        self.W = 2 * hidden + (self.FC + D if self.FC > 1 else 0)


L0 = Layer(1, "L0", 32, 128, 256)
L1 = Layer(2, "L1", 16, 512, 256)


def past(eng, passed):
    eng.sem_inc(passed, 1)


class Steps:

    def __init__(self, base):
        self.base, self.n = base, 0

    def one(self):
        self.n += 1
        return 1

    def all(self):
        return self.base + self.n


class Norm:

    def __init__(self, sb, n):
        self.bn, self.mv = sb(f"bn{n}", [ROWS, TILES, 6]), sb(f"mv{n}", [ROWS, TILES, 2])
        self.ve, self.rs = sb(f"ve{n}", [ROWS, TILES]), sb(f"rs{n}", [ROWS, TILES])


class Tables:

    def __init__(self, sb):
        self.cnt, self.up, self.nb = sb("t_cnt", [32, 1]), sb("t_up", [32, 1], I32), sb("t_nb", [32, 1])
        self.cb, self.ge, self.v = sb("t_cb", [32, 1]), sb("t_ge", [32, 192]), sb("t_v", [32, 2])
        self.er = sb("t_er", [1, 192], I32)
        self.rf, self.rr = sb("t_rf", [1, 192]), sb("t_rr", [1, 192], I32)
        self.fr = sb("t_fr", [1, 32], I32)


class TableSignals:

    def __init__(self, sem):
        self.cnt_ps = sem("cnt_ps")
        self.nb_ready = sem("nb_ready")
        self.cb_ps = sem("cb_ps")
        self.ge_ready = sem("ge_ready")
        self.tab_ps = sem("tab_ps")
        self.tables_ready = sem("tables_ready")
        self.pads_in = sem("pads_in")
        self.table_step = sem("table_step")


class LayerSignals:

    def __init__(self, sem, halves, n):
        self.htok_ready = sem(f"{n}_htok_ready")
        self.statsB = sem(f"{n}_statsB")
        self.rstdB = sem(f"{n}_rstdB")
        self.rows0_ready = sem(f"{n}_rows0_ready")
        self.rows1_ready = sem(f"{n}_rows1_ready")
        self.x2T_ps = sem(f"{n}_x2T_ps")
        self.x2T_ready = sem(f"{n}_x2T_ready")
        self.lg_ps = sem(f"{n}_lg_ps")
        self.top_ready = sem(f"{n}_top_ready")
        self.oh_ready = sem(f"{n}_oh_ready")
        self.rank_ps = sem(f"{n}_rank_ps")
        self.rank_read = sem(f"{n}_rank_read")
        self.slot_ready = sem(f"{n}_slot_ready")
        self.eg_ready = sem(f"{n}_eg_ready")
        self.gate_ready = sem(f"{n}_gate_ready")
        self.place_ready = sem(f"{n}_place_ready")
        self.dveR = sem(f"{n}_dveR")
        self.poolR = sem(f"{n}_poolR")
        self.scattered = halves(f"{n}_scattered")
        self.resid_out = halves(f"{n}_resid_out")


class BlockSignals:

    def __init__(self, sem, i0, j0, y0, first=None):
        self.i0, self.j0, self.y0 = i0, j0, y0
        if first is None:
            self.blk_in = [sem(f"blk_in{u}") for u in range(NB)]
            self.y_out = [sem(f"y_out{u}") for u in range(NB)]
            self.xT_ps, self.xT_ready = sem("bxT_ps"), sem("bxT_ready")
            self.h_ps, self.h_ready = sem("bh_ps"), sem("bh_ready")
            self.y_ps, self.y_ready = sem("by_ps"), sem("by_ready")
        else:
            self.blk_in, self.y_out = first.blk_in, first.y_out
            self.xT_ps, self.xT_ready = first.xT_ps, first.xT_ready
            self.h_ps, self.h_ready = first.h_ps, first.h_ready
            self.y_ps, self.y_ready = first.y_ps, first.y_ready


def build(nc, a, out):
    ctx = ExitStack()
    with ctx:
        def sb(name, shape, dt=F32):
            return ctx.enter_context(nc.sbuf_tensor(name, shape, dt))

        def part(tensor, p, at, n):
            return tensor[0:p, :, :].rearrange("p a b -> p (a b)")[:, at:at + n]

        def sem(name):
            return ctx.enter_context(nc.semaphore(name))

        def halves(name):
            return [sem(f"{name}{h}") for h in range(2)]

        def dram(name, shape):
            return nc.dram_tensor(name, shape, F32, kind="Internal").ap()

        lists = {l.name: dram(f"lists_{l.name}", [l.E * l.room + l.block, ROW]) for l in (L0, L1)}
        results = {l.name: dram(f"results_{l.name}", [TOKENS * TOP, D]) for l in (L0, L1)}
        resid = {l.name: dram(f"resid_{l.name}", [GROUPS, ROWS, TILES * D]) for l in (L0, L1)}

        ps = ctx.enter_context(nc.psum_tensor("ps", [128, 8, BANK], F32))
        psE = [ps[:, h, :] for h in range(2)]
        pair = [ps[:, 2 + 2 * n:4 + 2 * n, :].rearrange("p b n -> p (b n)") for n in range(3)]

        ident = sb("ident", [128, 128])
        w_emb = sb("w_emb", [128, KT, D])
        w_rest = sb("w_rest", [KREST, D])
        wq, wk, wv = sb("wq", [D, D]), sb("wk", [D, D]), sb("wv", [D, D])
        cols = sb("cols", [D, 4])
        bv_rows = sb("bv_rows", [SEQ, D])
        posT = sb("posT", [D, SEQ])
        causal = sb("causal", [SEQ, SEQ])
        selT = {"L0": sb("selT_L0", [D, L0.E]), "L1": sb("selT_L1", [D, L1.E])}
        rb_rows = sb("rb_rows", [ROWS, L1.E])
        ones = sb("ones", [128, 128])
        ones16 = sb("ones16", [128, 128], BF16)
        before16 = sb("before16", [128, 128], BF16)
        upto = sb("upto", [32, 32])
        iotaE = sb("iotaE", [ROWS, 32])
        iotaB = sb("iotaB", [32, 192])
        half_m = sb("half_m", [128, TILES])
        half_p = sb("half_p", [128, TILES])
        place0 = sb("place0", [ROWS, TILES, TOP])
        padrows = sb("padrows", [128, 2, ROW])
        kcol = sb("kcol", [128, 2])
        first0 = sb("first0", [128, GI, SEQ])
        decay = sb("decay", [128, GI, SEQ])

        xin = [[sb(f"xin{h}_{c}", [128, KC, GP]) for c in range(CHUNKS)] for h in range(2)]
        xrest = [sb(f"xrest{h}", [KREST, GP]) for h in range(2)]
        h0T = [sb(f"h0T{h}", [D, GI, SEQ]) for h in range(2)]
        x1T = [sb(f"x1T{h}", [D, GT]) for h in range(2)]
        QT, KTt = sb("QT", [D, GT]), sb("KT", [D, GT])
        V = [sb(f"V{h}", [SEQ, GI, D]) for h in range(2)]
        Sm = sb("Sm", [SEQ, GI, SEQ])
        Pr = [sb(f"Pr{h}", [SEQ, GI, SEQ]) for h in range(2)]
        smax = sb("smax", [SEQ, GI])
        ssum = sb("ssum", [SEQ, GI])
        u0T = sb("u0T", [D, GT])
        h1T = sb("h1T", [D, GT])
        atok = sb("atok", [ROWS, TILES, D])
        ntok = sb("ntok", [ROWS, TILES, D])
        LNA, LNB = Norm(sb, "A"), Norm(sb, "B")
        htok = [sb(f"htok{h}", [ROWS, TILES, D]) for h in range(2)]
        rows = [sb(f"rows{h}", [ROWS, TILES, TOP, ROW]) for h in range(2)]
        x2T = sb("x2T", [D, TILES, ROWS])
        lg = sb("lg", [ROWS, TILES, 32])
        top8 = sb("top8", [ROWS, TILES, 8])
        idx8 = sb("idx8", [ROWS, TILES, 8], U32)
        chosen = sb("chosen", [ROWS, TILES, TOP])
        oh = sb("oh", [ROWS, TILES, TOP, 32], BF16)
        ohs = sb("ohs", [ROWS, TILES, 32], BF16)
        seen = sb("seen", [ROWS, 32], BF16)
        added = sb("added", [ROWS, 32])
        pick = sb("pick", [ROWS, TILES, TOP, 32])
        rank = sb("rank", [ROWS, TILES, TOP])
        slots = [sb(f"slots{h}", [ROWS, TILES, TOP], U32) for h in range(2)]
        eg = sb("eg", [ROWS, TILES, TOP])
        gsum = sb("gsum", [ROWS, TILES])
        lgs = sb("lgs", [ROWS, TILES, 32])
        place = sb("place", [ROWS, TILES, TOP])
        tb = Tables(sb)
        wblk = [part(xin[u % 2][u // 4], 128, u // 2 % 2 * L1.W, L1.W) for u in range(NB)]
        xblk = [part(xin[u % 2][2], 128, u // 2 * 2 * ROW, 2 * ROW).rearrange("p (q w) -> p q w", q=2)
                for u in range(NB)]
        yblk = [part(xin[u % 2][2], 128, 8 * ROW + u // 2 * 2 * D, 2 * D).rearrange("p (q d) -> p q d", q=2)
                for u in range(NB)]
        xTb = [sb(f"xTb{h}", [D, 2 * 128]) for h in range(2)]
        hTb = [sb(f"hTb{h}", [128, 4, 256]) for h in range(2)]
        yin = [part(xin[h][1], ROWS, 0, TILES * TOP * D).rearrange("p (t k d) -> p t k d", t=TILES, k=TOP)
               for h in range(2)]
        h2tok, hin = ([part(xin[h][1], ROWS, n * TILES * D, TILES * D).rearrange("p (t d) -> p t d", t=TILES)
                       for h in range(2)] for n in (2, 3))
        fin = [part(xin[h][2], ROWS, 0, TILES * D).rearrange("p (t d) -> p t d", t=TILES) for h in range(2)]
        actx, sq = (part(xin[1][2], ROWS, n * TILES * D, TILES * D).rearrange("p (t d) -> p t d", t=TILES)
                    for n in (2, 3))
        cumT, ctxT = (part(xin[h][2], D, TILES * D, GT).rearrange("p (i t) -> p i t", i=GI) for h in range(2))
        xc = part(xin[0][2], D, 2 * TILES * D, GT).rearrange("p (i t) -> p i t", i=GI)
        ssq = sb("ssq", [ROWS, TILES])
        mag = sb("mag", [ROWS, TILES])

        w_emb_in = sem("w_emb_in")
        consts_in = sem("consts_in")
        made = sem("made")
        made_step = sem("made_step")
        consts_dve = sem("consts_dve")
        chunk_in = [[sem(f"chunk_in{h}_{c}") for c in range(CHUNKS)] for h in range(2)]
        chunk_used = [[sem(f"chunk_used{h}_{c}") for c in range(CHUNKS)] for h in range(2)]
        emb_ps = sem("emb_ps")
        h0T_ready = sem("h0T_ready")
        h0_ps = sem("h0_ps")
        atok_ready = sem("atok_ready")
        statsA = sem("statsA")
        rstdA = sem("rstdA")
        ntok_ready = sem("ntok_ready")
        xT_ps = sem("xT_ps")
        x1T_ready = sem("x1T_ready")
        q_ps, k_ps, v_ps, s_ps = sem("q_ps"), sem("k_ps"), sem("v_ps"), sem("s_ps")
        q_ready, k_ready, v_ready = sem("q_ready"), sem("k_ready"), sem("v_ready")
        s_read = sem("s_read")
        shifted = sem("shifted")
        exp_ready = sem("exp_ready")
        p_ready = sem("p_ready")
        read_ps = sem("read_ps")
        h1T_ready = sem("h1T_ready")
        hT_ps = sem("hT_ps")
        dveA = sem("dveA")
        dveB = sem("dveB")
        poolA = sem("poolA")

        T = TableSignals(sem)
        S = {l.name: LayerSignals(sem, halves, l.name) for l in (L0, L1)}
        K = {"L0": BlockSignals(sem, 0, 0, 0)}
        K["L1"] = BlockSignals(sem, L0.blocks, L0.blocks // NB, 16 * L0.Q * L0.blocks // NB, K["L0"])
        m_in = halves("m_in")
        m_free = halves("m_free")
        h2_ready, m_statsA, m_rstdA, m_ntok, m_xT_ps, m_xc = (sem(n) for n in (
            "h2_ready", "m_statsA", "m_rstdA", "m_ntok", "m_xT_ps", "m_xc"))
        ctx_ready, delta_ready, ctx_ps, delta_ps, ssq_ready, mag_ready, actx_ready = (sem(n) for n in (
            "ctx_ready", "delta_ready", "ctx_ps", "delta_ps", "ssq_ready", "mag_ready", "actx_ready"))
        dveM, poolM = sem("dveM"), sem("poolM")
        dve_passed, pool_passed = sem("dve_passed"), sem("pool_passed")
        y_biased = sem("y_biased")
        e_in = halves("e_in")
        e_ready = sem("e_ready")
        e_dve = sem("e_dve")
        e_out = halves("e_out")

        block = ctx.enter_context(nc.Block())

        def pairs(eng, body, n=GROUPS):
            for h in range(2):
                body(h, h, 0)
            with eng.Fori(1, n // 2) as j:
                for h in range(2):
                    body(2 * j + h, h, j)

        NCONST = 10

        def rounds(eng, l, body):
            for u in range(l.unroll):
                body(u, 0)
            with eng.Fori(1, l.blocks // l.unroll) as j:
                for u in range(l.unroll):
                    body(u, j)

        def sp_blocks(sp, l):
            s, k = S[l.name], K[l.name]
            sp.wait_ge(T.tables_ready, l.turn)
            sp.wait_ge(made, 1)
            pad = padrows[:, 0:l.Q, :].rearrange("p q w -> p (q w)")
            room = lists[l.name]
            with sp.Fori(0, l.E) as e:
                at = sp.value_load(tb.fr[0:1, bass.ds(e, 1)], min_val=0, max_val=l.E * l.room - l.block)
                sp.dma_start(room[bass.ds(at, l.block), :].rearrange("(p q) w -> p (q w)", q=l.Q), pad)\
                    .then_inc(T.pads_in, 16)
            sp.dma_start(room[l.E * l.room:, :].rearrange("(p q) w -> p (q w)", q=l.Q), pad)\
                .then_inc(T.pads_in, 16)
            sp.wait_ge(T.pads_in, 16 * (l.E + 1) + (16 * (L0.E + 1) if l is L1 else 0))
            for h in range(2):
                sp.wait_ge(s.scattered[h], 16 * TILES * TOP * GROUPS // 2)
            weights = a[f"w_{l.name}"]

            def load(u, j):
                i = l.unroll * j + u
                e = sp.value_load(tb.er[0:1, bass.ds(i, 1)], min_val=0, max_val=l.E - 1)
                r = sp.value_load(tb.rr[0:1, bass.ds(i, 1)], min_val=0, max_val=l.E * l.room)
                sp.wait_ge(k.y_out[u], k.y0 + 16 * l.Q * j)
                sp.dma_start(wblk[u][:, 0:l.W], weights[bass.ds(e * 128, 128), :]).then_inc(k.blk_in[u], 16)
                sp.dma_start(xblk[u][:, 0:l.Q, :].rearrange("p q w -> p (q w)"),
                             room[bass.ds(r, l.block), :].rearrange("(p q) w -> p (q w)", q=l.Q))\
                    .then_inc(k.blk_in[u], 16)

            rounds(sp, l, load)

        def sp_group_in(sp, name, g, h, y_in, h_in, got):
            sp.dma_start(yin[h].rearrange("p t k d -> p t (k d)"),
                         results[name].rearrange("(g t p k) d -> g p t (k d)", g=GROUPS, p=ROWS, t=TILES)[
                             bass.ds(g, 1), :, :, :].rearrange("o p t n -> (o p) t n")).then_inc(got, 16)
            sp.dma_start(h_in[h][:, :, :].rearrange("p t d -> p (t d)"),
                         resid[name][bass.ds(g, 1), :, :].rearrange("o p n -> (o p) n")).then_inc(got, 16)

        @block.sync
        def _(sp):
            def load_patches(g, h, j):
                for c in range(CHUNKS):
                    sp.wait_ge(chunk_used[h][c], j)
                    sp.dma_start(xin[h][c][:, :, :].rearrange("p k n -> p (k n)"),
                                 a["x_main"][bass.ds(g * CHUNKS + c, 1), :, :].rearrange("o p n -> (o p) n"))\
                        .then_inc(chunk_in[h][c], 16)
                    if c == CHUNKS - 1:
                        sp.dma_start(xrest[h][:, :], a["x_rest"][bass.ds(g, 1), :, :]
                                     .rearrange("o p n -> (o p) n")).then_inc(chunk_in[h][c], 16)
            pairs(sp, load_patches)
            sp_blocks(sp, L0)
            for u in range(NB):
                sp.wait_ge(K["L0"].y_out[u], 16 * L0.Q * L0.blocks // L0.unroll)
            for h in range(2):
                sp.wait_ge(S["L0"].resid_out[h], 16 * GROUPS // 2)

            def load_mid(g, h, j):
                sp.wait_ge(m_free[h], j)
                sp_group_in(sp, "L0", g, h, yin, hin, m_in[h])
            pairs(sp, load_mid)
            sp_blocks(sp, L1)
            for u in range(NB):
                sp.wait_ge(K["L1"].y_out[u], K["L1"].y0 + 16 * L1.Q * L1.blocks // L1.unroll)
            for h in range(2):
                sp.wait_ge(S["L1"].resid_out[h], 16 * GROUPS // 2)

            def load_end(g, h, j):
                sp.wait_ge(e_ready, 2 * j)
                sp_group_in(sp, "L1", g, h, yin, hin, e_in[h])
            pairs(sp, load_end)

        @block.tensor
        def _(pe):
            pe.wait_ge(w_emb_in, 32)

            def embed(g, h, j, first, end):
                for k in range(first, end):
                    c, n = divmod(k, KC)
                    if n == 0:
                        pe.wait_ge(chunk_in[h][c], (j + 1) * (32 if c == CHUNKS - 1 else 16))
                    mm = pe.matmul(psE[h], w_emb[:, k, :], xin[h][c][:, n, :], start=(k == 0), stop=False,
                                   skip_group_check=True)
                    if k == KT - 1:
                        mm = pe.matmul(psE[h], w_rest[:, :], xrest[h][:, :], start=False, stop=True,
                                       skip_group_check=True)
                    if n == KC - 1:
                        mm.then_inc(chunk_used[h][c], 1)

            def tok_from_T(srcT, p):
                for t in range(TILES):
                    mm = pe.transpose(pair[p][0:ROWS, t * 128:(t + 1) * 128], srcT[:, t * ROWS:(t + 1) * ROWS],
                                      ident[:, :])
                return mm

            def T_from_tok(tile, p):
                for t in range(TILES):
                    mm = pe.transpose(pair[p][:, t * 128:t * 128 + ROWS], tile(t), ident[0:ROWS, 0:ROWS])
                return mm

            def a1(g, h, j):
                pe.wait_ge(h0T_ready, g + 1)
                pe.wait_ge(v_ready, g)
                tok_from_T(h0T[h][:, :, :].rearrange("p i t -> p (i t)"), 0).then_inc(h0_ps, 1)

            def a2(g, h, j):
                pe.wait_ge(ntok_ready, g + 1)
                T_from_tok(lambda t: ntok[:, t, :], 0).then_inc(xT_ps, 1)

            def a3(g, h, j):
                pe.wait_ge(x1T_ready, g + 1)
                for n in range(2):
                    mm = pe.matmul(pair[0][:, n * BANK:n * BANK + HALF], wq[:, :], x1T[h][:, n * HALF:(n + 1) * HALF],
                                   start=True, stop=True)
                mm.then_inc(q_ps, 1)
                pe.wait_ge(s_read, g)
                for n in range(2):
                    mm = pe.matmul(pair[1][:, n * BANK:n * BANK + HALF], wk[:, :], x1T[h][:, n * HALF:(n + 1) * HALF],
                                   start=True, stop=True)
                mm.then_inc(k_ps, 1)

            def a4(g, h, j):
                pe.wait_ge(q_ready, g + 1)
                for i in range(GI):
                    mm = pe.matmul(pair[0][0:SEQ, i * D:(i + 1) * D], x1T[h][:, i * SEQ:(i + 1) * SEQ], wv[:, :],
                                   start=True, stop=True)
                mm.then_inc(v_ps, 1)
                pe.wait_ge(k_ready, g + 1)
                for i in range(GI):
                    c = i // 4 * BANK + i % 4 * SEQ
                    mm = pe.matmul(pair[1][0:SEQ, c:c + SEQ], KTt[:, i * SEQ:(i + 1) * SEQ],
                                   QT[:, i * SEQ:(i + 1) * SEQ], start=True, stop=True)
                mm.then_inc(s_ps, 1)

            def b1(g, h, j):
                pe.wait_ge(p_ready, g + 1)
                pe.wait_ge(v_ready, g + 1)
                pe.wait_ge(S["L0"].rank_read, g)
                for i in range(GI):
                    c = i // 4 * BANK + i % 4 * SEQ
                    mm = pe.matmul(pair[2][:, c:c + SEQ], V[h][:, i, :], Pr[h][:, i, :], start=True, stop=True)
                mm.then_inc(read_ps, 1)

            def b2(g, h, j):
                pe.wait_ge(h1T_ready, g + 1)
                tok_from_T(h1T[:, :], 2).then_inc(hT_ps, 1)

            def r1(l, g, h, j):
                s = S[l.name]
                pe.wait_ge(s.rows0_ready, g + 1)
                if l is L1:
                    pe.wait_ge(s.rank_read, g)
                T_from_tok(lambda t: rows[h][:, t, 0, 0:D], 2).then_inc(s.x2T_ps, 1)

            def r2(l, g, h, j):
                s = S[l.name]
                pe.wait_ge(s.x2T_ready, g + 1)
                for t in range(TILES):
                    mm = pe.matmul(pair[2][0:ROWS, t * l.E:(t + 1) * l.E], x2T[:, t, :], selT[l.name][:, :],
                                   start=True, stop=True)
                mm.then_inc(s.lg_ps, 1)

            def r3(l, g, h, j):
                s = S[l.name]
                pe.wait_ge(s.oh_ready, g + 1)
                out_ = pair[2][0:ROWS, 0:TILES * l.E].rearrange("p (t e) -> p t e", t=TILES)
                pe.matmul(out_, before16[0:ROWS, 0:ROWS], ohs[:, :, 0:l.E], start=True, stop=False,
                          skip_group_check=True)
                for t in range(TILES - 1):
                    pe.matmul(out_[:, t + 1:, :], ones16[0:ROWS, 0:ROWS],
                              ohs[:, t:t + 1, 0:l.E].to_broadcast([ROWS, TILES - 1 - t, l.E]),
                              start=False, stop=False, skip_group_check=True)
                pe.matmul(out_, ones16[0:ROWS, 0:ROWS],
                          seen[:, None, 0:l.E].to_broadcast([ROWS, TILES, l.E]),
                          start=False, stop=True, skip_group_check=True).then_inc(s.rank_ps, 1)

            def tables(l):
                s = S[l.name]
                pe.wait_ge(s.slot_ready, GROUPS)
                pe.matmul(pair[0][0:l.E, 0:1], seen[:, 0:l.E], ones16[0:ROWS, 0:1], start=True, stop=True)
                pe.matmul(pair[1][0:1, 0:l.E], ones16[0:ROWS, 0:1], seen[:, 0:l.E], start=True, stop=True)\
                    .then_inc(T.cnt_ps, 1)
                pe.wait_ge(T.nb_ready, l.turn)
                pe.matmul(pair[2][0:l.E, 0:1], upto[0:l.E, 0:l.E], tb.nb[0:l.E, :], start=True, stop=True)\
                    .then_inc(T.cb_ps, 1)
                pe.wait_ge(T.ge_ready, l.turn)
                pe.matmul(pair[0][0:1, 0:l.blocks], tb.v[0:l.E, 0:1], tb.ge[0:l.E, 0:l.blocks], start=True, stop=True)
                pe.matmul(pair[1][0:1, 0:l.blocks], tb.v[0:l.E, 1:2], tb.ge[0:l.E, 0:l.blocks], start=True, stop=True)\
                    .then_inc(T.tab_ps, 1)

            def expert_blocks(l):
                k = K[l.name]
                U = l.unroll
                n_tok = l.block

                def bank_x(i2):
                    return ps[:, i2, 0:n_tok]

                def bank_h(i2, f):
                    b = 2 + 2 * i2 + f // 2
                    return ps[:, b, f % 2 * n_tok:f % 2 * n_tok + n_tok]

                def turn(u, n, j):
                    return (u + n) % U, j + (u + n) // U

                def t1(u, j, n):
                    b, jj = turn(u, n, j)
                    pe.wait_ge(k.blk_in[b], 32 * (k.j0 + jj + 1))
                    for q in range(l.Q):
                        mm = pe.transpose(ps[:, (u + n) % 2, q * 128:(q + 1) * 128], xblk[b][:, q, 0:D], ident[:, :])
                    mm.then_inc(k.xT_ps, 1)

                def t2(u, j, n):
                    b, jj = turn(u, n, j)
                    i = U * j + u + n
                    pe.wait_ge(k.xT_ready, k.i0 + i + 1)
                    for f in range(l.FC):
                        mm = pe.matmul(bank_h(i_par(u, n), f), wblk[b][:, f * 128:(f + 1) * 128],
                                       xTb[i_par(u, n)][:, 0:n_tok], start=True, stop=True)
                    mm.then_inc(k.h_ps, 1)

                def t3(u, j, n):
                    b, jj = turn(u, n, j)
                    i = U * j + u + n
                    p2 = i_par(u, n)
                    pe.wait_ge(k.h_ready, k.i0 + i + 1)
                    if not (isinstance(i, int) and i < 2):
                        pe.wait_ge(k.y_ready, k.i0 + i - 1)
                    w2 = wblk[b][:, l.FC * 128:2 * l.FC * 128]
                    for q in range(l.Q):
                        o = ps[:, 6 + p2, q * D:(q + 1) * D]
                        for f in range(l.FC):
                            mm = pe.matmul(o, hTb[p2][:, f, q * 128:(q + 1) * 128], w2[:, f * D:(f + 1) * D],
                                           start=(f == 0), stop=(f == l.FC - 1))
                    mm.then_inc(k.y_ps, 1)

                def i_par(u, n):
                    return (u + n) % 2

                rounds = l.blocks // U
                t1(0, 0, 0)
                t1(0, 0, 1)
                t2(0, 0, 0)

                def step(u, j, last):
                    if not (last and u + 2 >= U):
                        t1(u, j, 2)
                    if not (last and u + 1 >= U):
                        t2(u, j, 1)
                    t3(u, j, 0)
                for u in range(U):
                    step(u, 0, False)
                with pe.Fori(1, rounds - 1) as j:
                    for u in range(U):
                        step(u, j, False)
                for u in range(U):
                    step(u, rounds - 1, True)

            def step(g, h, j, ahead_a, ahead_e):
                o, jo = 1 - h, j + h

                def tiles(first, end):
                    if ahead_e:
                        embed(g + 2, h, j + 1, first, end)
                tiles(0, 3)
                b1(g, h, j)
                if ahead_a:
                    a1(g + 1, o, jo)
                tiles(3, 5)
                b2(g, h, j)
                tiles(5, 8)
                if ahead_a:
                    a2(g + 1, o, jo)
                tiles(8, 10)
                if ahead_a:
                    a3(g + 1, o, jo)
                r1(L0, g, h, j)
                tiles(10, 12)
                if ahead_a:
                    a4(g + 1, o, jo)
                r2(L0, g, h, j)
                tiles(12, KT)
                r3(L0, g, h, j)

            embed(0, 0, 0, 0, KT)
            pe.wait_ge(consts_in, 16 * NCONST)
            pe.wait_ge(made, 1)
            pe.wait_ge(consts_dve, 1)
            for f, first in ((a1, 0), (a2, 6), (a3, 10), (a4, 13)):
                f(0, 0, 0)
                embed(1, 1, 0, first, {0: 6, 6: 10, 10: 13, 13: KT}[first])
            for h in range(2):
                step(h, h, 0, True, True)
            with pe.Fori(1, GROUPS // 2 - 1) as j:
                for h in range(2):
                    step(2 * j + h, h, j, True, True)
            j = GROUPS // 2 - 1
            step(2 * j, 0, j, True, False)
            step(2 * j + 1, 1, j, False, False)
            tables(L0)
            expert_blocks(L0)

            def c1(g, h, j):
                pe.wait_ge(m_ntok, g + 1)
                pe.wait_ge(actx_ready, g)
                T_from_tok(lambda t: ntok[:, t, :], 0).then_inc(m_xT_ps, 1)

            def c2(g, h, j):
                pe.wait_ge(ctx_ready, g + 1)
                tok_from_T(ctxT[:, :, :].rearrange("p i t -> p (i t)"), 0).then_inc(ctx_ps, 1)

            def c3(g, h, j):
                pe.wait_ge(delta_ready, g + 1)
                pe.wait_ge(ssq_ready, g)
                tok_from_T(cumT[:, :, :].rearrange("p i t -> p (i t)"), 1).then_inc(delta_ps, 1)

            def mid_step(g, h, j, ahead):
                o, jo = 1 - h, j + h
                if ahead:
                    c1(g + 1, o, jo)
                r1(L1, g, h, j)
                if ahead:
                    c2(g + 1, o, jo)
                r2(L1, g, h, j)
                if ahead:
                    c3(g + 1, o, jo)
                r3(L1, g, h, j)

            for f in (c1, c2, c3):
                f(0, 0, 0)
            for h in range(2):
                mid_step(h, h, 0, True)
            with pe.Fori(1, GROUPS // 2 - 1) as j:
                for h in range(2):
                    mid_step(2 * j + h, h, j, True)
            j = GROUPS // 2 - 1
            mid_step(2 * j, 0, j, True)
            mid_step(2 * j + 1, 1, j, False)
            tables(L1)
            expert_blocks(L1)

        @block.scalar
        def _(act):
            act.dma_start(w_emb[:, :, :].rearrange("p k d -> p (k d)"), a["w_main"]).then_inc(w_emb_in, 16)
            act.dma_start(w_rest[:, :], a["w_rest"]).then_inc(w_emb_in, 16)
            for dst, src in ((wq[:, :], a["wq"]), (wk[:, :], a["wk"]), (wv[:, :], a["wv"]), (cols[:, :], a["cols"]),
                             (bv_rows[:, :], a["bv"].to_broadcast([SEQ, D])), (posT[:, :], a["posT"]),
                             (selT["L0"][:, :], a["selT0"]), (selT["L1"][:, :], a["selT1"]),
                             (rb_rows[:, :], a["rb"].to_broadcast([ROWS, L1.E])),
                             (kcol[:, 0:1], a["k"].to_broadcast([128, 1]))):
                act.dma_start(dst, src).then_inc(consts_in, 16)
            act.wait_ge(consts_in, 16 * NCONST)
            act.activation(kcol[:, 1:2], kcol[:, 0:1], ACT.Exp).then_inc(exp_ready, 1)

            def copy(dst, src):
                return act.activation(dst, src, ACT.Copy)

            def flat(tile):
                return tile.rearrange("p t d -> p (t d)")

            def a1(g, h, j):
                act.wait_ge(h0_ps, g + 1)
                act.wait_ge(ntok_ready, g)
                copy(flat(atok[:, :, :]), pair[0][0:ROWS, 0:TILES * D]).then_inc(atok_ready, 1)

            def a2(g, h, j):
                act.wait_ge(xT_ps, g + 1)
                copy(x1T[h][:, :].rearrange("p (t r) -> p t r", t=TILES),
                     pair[0][:, 0:TILES * 128].rearrange("p (t r) -> p t r", t=TILES)[:, :, 0:ROWS])\
                    .then_inc(x1T_ready, 1)

            def a3(g, h, j):
                act.wait_ge(q_ps, g + 1)
                act.activation(QT[:, :].rearrange("p (n r) -> p n r", n=2),
                               pair[0].rearrange("p (n r) -> p n r", n=2)[:, :, 0:HALF],
                               ACT.Identity, bias=cols[:, 1:2]).then_inc(q_ready, 1)
                act.wait_ge(k_ps, g + 1)
                act.wait_ge(s_ps, g)
                act.activation(KTt[:, :].rearrange("p (n r) -> p n r", n=2),
                               pair[1].rearrange("p (n r) -> p n r", n=2)[:, :, 0:HALF],
                               ACT.Identity, bias=cols[:, 2:3]).then_inc(k_ready, 1)

            def a4(g, h, j):
                act.wait_ge(shifted, g + 1)
                act.activation(Pr[h][:, :, :].rearrange("p i t -> p (i t)"), Sm[:, :, :].rearrange("p i t -> p (i t)"),
                               ACT.Exp).then_inc(exp_ready, 1)

            def b2(g, h, j):
                s = S["L0"]
                act.wait_ge(hT_ps, g + 1)
                act.wait_ge(s.resid_out[h], 16 * j)
                copy(flat(htok[h][:, :, :]), pair[2][0:ROWS, 0:TILES * D]).then_inc(s.htok_ready, 1)
                act.wait_ge(s.htok_ready, g + 1)
                act.dma_start(resid["L0"][bass.ds(g, 1), :, :].rearrange("o p n -> (o p) n"),
                              flat(htok[h][:, :, :])).then_inc(s.resid_out[h], 16)

            def r1(l, g, h, j):
                s = S[l.name]
                act.wait_ge(s.x2T_ps, g + 1)
                copy(x2T[:, :, :], pair[2][:, 0:TILES * 128].rearrange("p (t r) -> p t r", t=TILES)[:, :, 0:ROWS])\
                    .then_inc(s.x2T_ready, 1)
                act.wait_ge(s.rows0_ready, g + 1)
                copy(rows[h][:, :, 1, 0:D], rows[h][:, :, 0, 0:D]).then_inc(s.rows1_ready, 1)

            def r2(l, g, h, j):
                s = S[l.name]
                act.wait_ge(s.top_ready, g + 1)
                if l is L0:
                    act.activation(eg[:, :, :], top8[:, :, 0:TOP], ACT.Exp, scale=-1.0).then_inc(s.eg_ready, 1)
                else:
                    act.activation(lgs[:, :, 0:l.E], lgs[:, :, 0:l.E], ACT.Exp)
                    act.activation(eg[:, :, :], eg[:, :, :], ACT.Exp).then_inc(s.eg_ready, 1)

            def front_step(g, h, j, ahead):
                o, jo = 1 - h, j + h
                if ahead:
                    a1(g + 1, o, jo)
                b2(g, h, j)
                if ahead:
                    a2(g + 1, o, jo)
                    a3(g + 1, o, jo)
                r1(L0, g, h, j)
                if ahead:
                    a4(g + 1, o, jo)
                r2(L0, g, h, j)

            for f in (a1, a2, a3, a4):
                f(0, 0, 0)
            for h in range(2):
                front_step(h, h, 0, True)
            with act.Fori(1, GROUPS // 2 - 1) as j:
                for h in range(2):
                    front_step(2 * j + h, h, j, True)
            j = GROUPS // 2 - 1
            front_step(2 * j, 0, j, True)
            front_step(2 * j + 1, 1, j, False)

            def expert_blocks(l):
                k = K[l.name]
                U = l.unroll

                def xT(u, j, n):
                    i = U * j + u + n
                    p2 = (u + n) % 2
                    act.wait_ge(k.xT_ps, k.i0 + i + 1)
                    if not (isinstance(i, int) and i < 2):
                        act.wait_ge(k.h_ps, k.i0 + i - 1)
                    copy(xTb[p2][:, 0:l.block], ps[:, p2, 0:l.block]).then_inc(k.xT_ready, 1)

                def gelu(u, j, n):
                    i = U * j + u + n
                    p2 = (u + n) % 2
                    b = (u + n) % U
                    act.wait_ge(k.h_ps, k.i0 + i + 1)
                    if not (isinstance(i, int) and i < 2):
                        act.wait_ge(k.y_ps, k.i0 + i - 1)
                    for f in range(l.FC):
                        b1 = wblk[b][:, 2 * l.FC * 128 + f:2 * l.FC * 128 + f + 1]
                        ins = act.activation(hTb[p2][:, f, 0:l.block],
                                             ps[:, 2 + 2 * p2 + f // 2, f % 2 * l.block:(f % 2 + 1) * l.block],
                                             ACT.Gelu, bias=b1)
                    ins.then_inc(k.h_ready, 1)

                f = xT if l is L0 else gelu
                lead = 2 if l is L0 else 1
                for n in range(lead):
                    f(0, 0, n)
                for u in range(U):
                    f(u, 0, lead)
                with act.Fori(1, l.blocks // U - 1) as j:
                    for u in range(U):
                        f(u, j, lead)
                for u in range(U - lead):
                    f(u, l.blocks // U - 1, lead)

            expert_blocks(L0)

            def c1(g, h, j):
                act.wait_ge(m_xT_ps, g + 1)
                act.wait_ge(delta_ready, g)
                act.wait_ge(ctx_ready, g)
                copy(xc[:, :, :].rearrange("p i t -> p (i t)").rearrange("p (t r) -> p t r", t=TILES),
                     pair[0][:, 0:TILES * 128].rearrange("p (t r) -> p t r", t=TILES)[:, :, 0:ROWS])\
                    .then_inc(m_xc, 1)

            def c2(g, h, j):
                act.wait_ge(delta_ps, g + 1)
                act.wait_ge(mag_ready, g)
                for t in range(TILES):
                    ins = act.activation(sq[:, t, :], pair[1][0:ROWS, t * D:(t + 1) * D], ACT.Square,
                                         accum_out=ssq[:, t:t + 1])
                ins.then_inc(ssq_ready, 1)
                act.wait_ge(mag_ready, g + 1)
                act.wait_ge(ctx_ps, g + 1)
                act.wait_ge(S["L1"].htok_ready, g)
                for t in range(TILES):
                    ins = act.activation(actx[:, t, :], pair[0][0:ROWS, t * D:(t + 1) * D], ACT.Abs,
                                         scale=mag[:, t:t + 1])
                ins.then_inc(actx_ready, 1)

            def c3(g, h, j):
                s = S["L1"]
                act.wait_ge(s.htok_ready, g + 1)
                act.dma_start(resid["L1"][bass.ds(g, 1), :, :].rearrange("o p n -> (o p) n"),
                              flat(htok[h][:, :, :])).then_inc(s.resid_out[h], 16)

            def mid_step(g, h, j, ahead):
                o, jo = 1 - h, j + h
                if ahead:
                    c1(g + 1, o, jo)
                r1(L1, g, h, j)
                r2(L1, g, h, j)
                if ahead:
                    c2(g + 1, o, jo)
                    c3(g + 1, o, jo)

            for f in (c1, c2, c3):
                f(0, 0, 0)
            for h in range(2):
                mid_step(h, h, 0, True)
            with act.Fori(1, GROUPS // 2 - 1) as j:
                for h in range(2):
                    mid_step(2 * j + h, h, j, True)
            j = GROUPS // 2 - 1
            mid_step(2 * j, 0, j, True)
            mid_step(2 * j + 1, 1, j, False)
            expert_blocks(L1)
            def store(g, h, j):
                act.wait_ge(e_ready, g + 1)
                act.dma_start(out.rearrange("(g t p) d -> g p t d", g=GROUPS, p=ROWS)[bass.ds(g, 1), :, :, :]
                              .rearrange("o p t d -> (o p) t d"), fin[h][:, :, :]).then_inc(e_out[h], 16)
            pairs(act, store)
            for h in range(2):
                act.wait_ge(e_out[h], 16 * GROUPS // 2)

        @block.vector
        def _(dve):
            dve.wait_ge(consts_in, 16 * NCONST)
            dve.wait_ge(made, 1)
            st = Steps(1)
            for h in range(2):
                ins = dve.tensor_scalar(h0T[h][:, :, 0:1], h0T[h][:, :, 0:1], cols[:, 3:4], posT[:, 0:1],
                                        ALU.add, ALU.mult)
            ins.then_inc(consts_dve, 1)

            def norm_stats(ln, x, st, step, stats):
                for t in range(TILES):
                    ins = dve.bn_stats(ln.bn[:, t, :], x[:, t, :])
                ins.then_inc(step, st.one())
                dve.wait_ge(step, st.all())
                past(dve, dve_passed)
                for t in range(TILES):
                    ins = dve.bn_aggr(ln.mv[:, t, :], ln.bn[:, t, :])
                ins.then_inc(stats, 1)

            def norm_apply(ln, x, y):
                for t in range(TILES):
                    ins = dve.tensor_scalar(y(t), x[:, t, :], ln.mv[:, t, 0:1], ln.rs[:, t:t + 1],
                                            ALU.subtract, ALU.mult)
                return ins

            NA, NBB, NR = 5, 1, {"L0": 9, "L1": 12}

            def e0(g, h, j):
                dve.wait_ge(chunk_used[h][CHUNKS - 1], j + 1)
                dve.scalar_tensor_tensor(h0T[h][:, :, 1:], psE[h].rearrange("p (i n) -> p i n", i=GI), cols[:, 0:1],
                                         posT[:, None, 1:].to_broadcast([D, GI, PATCHES]), ALU.add, ALU.mult)\
                    .then_inc(h0T_ready, 1)

            def a1(g, h, j):
                st = Steps(NA * g)
                dve.wait_ge(atok_ready, g + 1)
                norm_stats(LNA, atok, st, dveA, statsA)

            def a1_apply(g, h, j):
                dve.wait_ge(rstdA, g + 1)
                dve.wait_ge(statsA, g + 1)
                dve.wait_ge(xT_ps, g)
                norm_apply(LNA, atok, lambda t: ntok[:, t, :]).then_inc(ntok_ready, 1)

            def a2(g, h, j):
                dve.wait_ge(v_ps, g + 1)
                dve.tensor_tensor(V[h][:, :, :], pair[0][0:SEQ, :].rearrange("p (i d) -> p i d", i=GI),
                                  bv_rows[:, None, :].to_broadcast([SEQ, GI, D]), ALU.add).then_inc(v_ready, 1)

            def a3(g, h, j):
                st = Steps(NA * g + 1)
                dve.wait_ge(s_ps, g + 1)
                dve.wait_ge(exp_ready, g + 1)
                S4 = Sm[:, :, :].rearrange("p (n i) t -> p n i t", n=2)
                pv = pair[1][0:SEQ, :].rearrange("p (n r) -> p n r", n=2)[:, :, 0:HALF]\
                    .rearrange("p n (i t) -> p n i t", i=4)
                for n in range(2):
                    ins = dve.tensor_tensor(S4[:, n], pv[:, n], causal[:, None, :].to_broadcast([SEQ, 4, SEQ]),
                                            ALU.add)
                ins.then_inc(s_read, 1)
                dve.wait_ge(s_read, g + 1)
                dve.tensor_reduce(smax[:, :], Sm[:, :, :], X, ALU.max).then_inc(dveA, st.one())
                dve.wait_ge(dveA, st.all())
                dve.tensor_tensor(Sm[:, :, :], Sm[:, :, :], smax[:, :, None].to_broadcast([SEQ, GI, SEQ]),
                                  ALU.subtract).then_inc(shifted, 1)

            def a4(g, h, j):
                st = Steps(NA * g + 2)
                dve.wait_ge(exp_ready, g + 2)
                dve.tensor_reduce(ssum[:, :], Pr[h][:, :, :], X, ALU.add).then_inc(dveA, st.one())
                dve.wait_ge(dveA, st.all())
                dve.reciprocal(ssum[:, :], ssum[:, :]).then_inc(dveA, st.one())
                dve.wait_ge(dveA, st.all())
                dve.tensor_scalar(ssum[:, :], ssum[:, :], float(D) ** -0.5, None, ALU.mult).then_inc(dveA, st.one())
                dve.wait_ge(dveA, st.all())
                dve.tensor_tensor(Pr[h][:, :, :], Pr[h][:, :, :], ssum[:, :, None].to_broadcast([SEQ, GI, SEQ]),
                                  ALU.mult).then_inc(p_ready, 1)

            def b1(g, h, j):
                st = Steps(NBB * g)
                dve.wait_ge(read_ps, g + 1)
                dve.wait_ge(x1T_ready, g + 1)
                dve.wait_ge(hT_ps, g)
                dve.tensor_tensor(u0T[:, :], h0T[h][:, :, :].rearrange("p i t -> p (i t)"), x1T[h][:, :],
                                            ALU.add).then_inc(dveB, st.one())
                dve.wait_ge(dveB, st.all())
                dve.tensor_tensor(h1T[:, :].rearrange("p (n r) -> p n r", n=2),
                                  u0T[:, :].rearrange("p (n r) -> p n r", n=2),
                                  pair[2].rearrange("p (n r) -> p n r", n=2)[:, :, 0:HALF], ALU.add)\
                    .then_inc(h1T_ready, 1)

            def r1(l, g, h, j):
                s = S[l.name]
                st = Steps(NR[l.name] * g)
                dve.wait_ge(s.htok_ready, g + 1)
                norm_stats(LNB, htok[h], st, s.dveR, s.statsB)

            def r1_apply(l, g, h, j):
                s = S[l.name]
                dve.wait_ge(s.rstdB, g + 1)
                dve.wait_ge(s.statsB, g + 1)
                dve.wait_ge(s.scattered[h], 16 * TILES * TOP * j)
                norm_apply(LNB, htok[h], lambda t: rows[h][:, t, 0, 0:D]).then_inc(s.rows0_ready, 1)

            def r2(l, g, h, j):
                s = S[l.name]
                st = Steps(NR[l.name] * g + 1)
                E = l.E
                dve.wait_ge(s.lg_ps, g + 1)
                logit = pair[2][0:ROWS, 0:TILES * E].rearrange("p (t e) -> p t e", t=TILES)
                if l is L0:
                    dve.tensor_copy(lg[:, :, 0:E], logit).then_inc(s.dveR, st.one())
                else:
                    dve.tensor_tensor(lg[:, :, 0:E], logit,
                                                rb_rows[:, None, :].to_broadcast([ROWS, TILES, E]), ALU.add).then_inc(s.dveR, st.one())
                dve.wait_ge(s.dveR, st.all())
                dve.wait_ge(s.eg_ready, g)
                past(dve, dve_passed)
                for t in range(TILES):
                    ins = dve.max(top8[:, t, :], lg[:, t, 0:E])
                if l is L0:
                    ins.then_inc(s.top_ready, 1)
                    dve.wait_ge(s.top_ready, g + 1)
                else:
                    ins.then_inc(s.dveR, st.one())
                    dve.wait_ge(s.dveR, st.all())
                if l is L1:
                    dve.tensor_tensor(lgs[:, :, 0:E], lg[:, :, 0:E],
                                                top8[:, :, 0:1].to_broadcast([ROWS, TILES, E]), ALU.subtract).then_inc(s.dveR, st.one())
                    dve.tensor_tensor(eg[:, :, :], top8[:, :, 0:TOP], top8[:, :, 0:1].to_broadcast([ROWS, TILES, TOP]),
                                      ALU.subtract).then_inc(s.top_ready, 1)
                past(dve, dve_passed)
                for t in range(TILES):
                    ins = dve.max_index(idx8[:, t, :], top8[:, t, :], lg[:, t, 0:E])
                ins.then_inc(s.dveR, st.one())
                dve.wait_ge(s.dveR, st.all())
                dve.tensor_copy(chosen[:, :, :], idx8[:, :, 0:TOP]).then_inc(s.dveR, st.one())
                dve.wait_ge(s.dveR, st.all())
                for k in range(TOP):
                    ins = dve.tensor_tensor(oh[:, :, k, 0:E], iotaE[:, None, 0:E].to_broadcast([ROWS, TILES, E]),
                                            chosen[:, :, k:k + 1].to_broadcast([ROWS, TILES, E]), ALU.is_equal)
                ins.then_inc(s.dveR, st.one())
                dve.wait_ge(s.dveR, st.all())
                dve.wait_ge(s.rank_ps, g)
                dve.tensor_tensor(ohs[:, :, 0:E], oh[:, :, 0, 0:E], oh[:, :, 1, 0:E], ALU.add).then_inc(s.oh_ready, 1)
                dve.wait_ge(s.eg_ready, g + 1)
                if l is L0:
                    dve.tensor_scalar(eg[:, :, :], eg[:, :, :], 1.0, None, ALU.add).then_inc(s.dveR, st.one())
                    dve.wait_ge(s.dveR, st.all())
                    dve.reciprocal(rows[h][:, :, :, GATE], eg[:, :, :]).then_inc(s.gate_ready, 1)
                else:
                    dve.tensor_reduce(gsum[:, :], lgs[:, :, 0:E], X, ALU.add).then_inc(s.dveR, st.one())
                    dve.wait_ge(s.dveR, st.all())
                    dve.reciprocal(gsum[:, :], gsum[:, :]).then_inc(s.dveR, st.one())
                    dve.wait_ge(s.dveR, st.all())
                    dve.tensor_tensor(rows[h][:, :, :, GATE], eg[:, :, :],
                                      gsum[:, :, None].to_broadcast([ROWS, TILES, TOP]), ALU.mult)\
                        .then_inc(s.gate_ready, 1)
                return st

            def r3(l, g, h, j, st):
                s = S[l.name]
                E = l.E
                dve.wait_ge(s.oh_ready, g + 1)
                dve.tensor_reduce(added[:, 0:E], ohs[:, :, 0:E].rearrange("p t e -> p e t"), X, ALU.add).then_inc(s.dveR, st.one())
                dve.wait_ge(s.rank_ps, g + 1)
                rk = pair[2][0:ROWS, 0:TILES * E].rearrange("p (t e) -> p t e", t=TILES)
                for k in range(TOP):
                    ins = dve.tensor_tensor(pick[:, :, k, 0:E], rk, oh[:, :, k, 0:E], ALU.mult)
                ins.then_inc(s.rank_read, 1)
                dve.wait_ge(s.dveR, st.all())
                dve.tensor_tensor(seen[:, 0:E], seen[:, 0:E], added[:, 0:E], ALU.add).then_inc(s.dveR, st.one())
                dve.wait_ge(s.dveR, st.all())
                dve.tensor_reduce(rank[:, :, :], pick[:, :, :, 0:E], X, ALU.add).then_inc(s.dveR, st.one())
                dve.wait_ge(s.dveR, st.all())
                dve.scalar_tensor_tensor(slots[h][:, :, :], chosen[:, :, :], float(l.room), rank[:, :, :],
                                         ALU.mult, ALU.add).then_inc(s.slot_ready, 1)
                dve.wait_ge(s.slot_ready, g + 1)

            def front_step(g, h, j, ahead_a, ahead_e):
                o, jo = 1 - h, j + h
                b1(g, h, j)
                if ahead_a:
                    a1(g + 1, o, jo)
                r1(L0, g, h, j)
                if ahead_a:
                    a1_apply(g + 1, o, jo)
                r1_apply(L0, g, h, j)
                if ahead_a:
                    a2(g + 1, o, jo)
                    a3(g + 1, o, jo)
                st = r2(L0, g, h, j)
                if ahead_a:
                    a4(g + 1, o, jo)
                if ahead_e:
                    e0(g + 2, h, j + 1)
                r3(L0, g, h, j, st)
                assert st.n + 1 == NR["L0"], st.n

            dve.wait_ge(made, 1)
            dve.wait_ge(consts_dve, 1)
            e0(0, 0, 0)
            for f in (a1, a1_apply, a2, a3, a4):
                f(0, 0, 0)
            e0(1, 1, 0)
            for h in range(2):
                front_step(h, h, 0, True, True)
            with dve.Fori(1, GROUPS // 2 - 1) as j:
                for h in range(2):
                    front_step(2 * j + h, h, j, True, True)
            j = GROUPS // 2 - 1
            front_step(2 * j, 0, j, True, False)
            front_step(2 * j + 1, 1, j, False, False)

            def tables(l):
                s = S[l.name]
                E, n = l.E, l.blocks
                st = Steps(9 * (l.turn - 1))

                def link(ins):
                    ins.then_inc(T.table_step, st.one())
                    dve.wait_ge(T.table_step, st.all())
                dve.wait_ge(T.cnt_ps, l.turn)
                link(dve.tensor_copy(tb.cnt[0:E, :], pair[0][0:E, 0:1]))
                link(dve.scalar_tensor_tensor(tb.fr[:, 0:E], iotaB[0:1, 0:E], float(l.room), pair[1][0:1, 0:E],
                                              ALU.mult, ALU.add))
                link(dve.tensor_scalar(tb.up[0:E, :], tb.cnt[0:E, :], float(l.block - 1), None, ALU.add))
                link(dve.tensor_scalar(tb.up[0:E, :], tb.up[0:E, :], l.shift, None, ALU.arith_shift_right))
                dve.tensor_copy(tb.nb[0:E, :], tb.up[0:E, :]).then_inc(T.nb_ready, 1)
                dve.wait_ge(T.nb_ready, l.turn)
                link(dve.tensor_scalar(tb.v[0:E, 1:2], tb.nb[0:E, :], float(-l.block), float(l.room), ALU.mult, ALU.add))
                link(dve.memset(tb.v[0:E, 0:1], 1.0))
                dve.wait_ge(T.cb_ps, l.turn)
                link(dve.tensor_copy(tb.cb[0:E, :], pair[2][0:E, 0:1]))
                dve.tensor_scalar(tb.ge[0:E, 0:n], iotaB[0:E, 0:n], tb.cb[0:E, :], None, ALU.is_ge)\
                    .then_inc(T.ge_ready, 1)
                dve.wait_ge(T.tab_ps, l.turn)
                link(dve.tensor_scalar(tb.er[:, 0:n], pair[0][0:1, 0:n], float(E - 1), None, ALU.min))
                link(dve.scalar_tensor_tensor(tb.rf[:, 0:n], iotaB[0:1, 0:n], float(l.block), pair[1][0:1, 0:n],
                                              ALU.mult, ALU.add))
                dve.tensor_scalar(tb.rr[:, 0:n], tb.rf[:, 0:n], float(E * l.room), None, ALU.min)\
                    .then_inc(T.tables_ready, 1)
                assert st.n == 9, st.n

            tables(L0)

            def expert_blocks(l):
                k = K[l.name]
                U = l.unroll

                def relu(u, j, n):
                    i = U * j + u + n
                    p2 = (u + n) % 2
                    dve.wait_ge(k.h_ps, k.i0 + i + 1)
                    if not (isinstance(i, int) and i < 2):
                        dve.wait_ge(k.y_ps, k.i0 + i - 1)
                    dve.tensor_scalar(hTb[p2][:, 0, 0:l.block], ps[:, 2 + 2 * p2, 0:l.block], 0.0, None, ALU.max)\
                        .then_inc(k.h_ready, 1)

                def xT(u, j, n):
                    i = U * j + u + n
                    p2 = (u + n) % 2
                    dve.wait_ge(k.xT_ps, k.i0 + i + 1)
                    if not (isinstance(i, int) and i < 2):
                        dve.wait_ge(k.h_ps, k.i0 + i - 1)
                    dve.tensor_copy(xTb[p2][:, 0:l.block], ps[:, p2, 0:l.block]).then_inc(k.xT_ready, 1)

                def gated(u, j):
                    i = U * j + u
                    p2 = u % 2
                    dve.wait_ge(k.y_ps, k.i0 + i + 1)
                    dve.wait_ge(k.blk_in[u], 32 * (k.j0 + j + 1))
                    dve.wait_ge(k.y_out[u], k.y0 + 16 * l.Q * j)
                    y = ps[:, 6 + p2, 0:l.Q * D].rearrange("p (q d) -> p q d", q=l.Q)
                    gate = xblk[u][:, 0:l.Q, GATE:GATE + 1].to_broadcast([128, l.Q, D])
                    if l.FC > 1:
                        dve.tensor_tensor(yblk[u][:, :, :], y,
                                          wblk[u][:, None, l.W - D:l.W].to_broadcast([128, l.Q, D]), ALU.add)\
                            .then_inc(y_biased, 1)
                        dve.wait_ge(y_biased, i + 1)
                        y = yblk[u][:, :, :]
                    dve.tensor_tensor(yblk[u][:, :, :], y, gate, ALU.mult).then_inc(k.y_ready, 1)

                f, lead = (relu, 1) if l is L0 else (xT, 2)

                def step(u, j, last):
                    if not (last and u + lead >= U):
                        f(u, j, lead)
                    gated(u, j)
                for n in range(lead):
                    f(0, 0, n)
                for u in range(U):
                    step(u, 0, False)
                with dve.Fori(1, l.blocks // U - 1) as j:
                    for u in range(U):
                        step(u, j, False)
                for u in range(U):
                    step(u, l.blocks // U - 1, True)

            expert_blocks(L0)

            def c0(g, h, j):
                st = Steps(2 * g)
                dve.wait_ge(m_in[h], 32 * (j + 1))
                dve.tensor_tensor(h2tok[h][:, :, :], yin[h][:, :, 0, :], yin[h][:, :, 1, :], ALU.add).then_inc(dveM, st.one())
                dve.wait_ge(dveM, st.all())
                dve.tensor_tensor(h2tok[h][:, :, :], h2tok[h][:, :, :], hin[h][:, :, :], ALU.add)\
                    .then_inc(m_free[h], 1)
                dve.wait_ge(m_free[h], j + 1)
                norm_stats(LNA, h2tok[h], st, dveM, m_statsA)

            def c0_apply(g, h, j):
                dve.wait_ge(m_rstdA, g + 1)
                dve.wait_ge(m_statsA, g + 1)
                dve.wait_ge(m_xT_ps, g)
                norm_apply(LNA, h2tok[h], lambda t: ntok[:, t, :]).then_inc(m_ntok, 1)

            def c1(g, h, j):
                dve.wait_ge(m_xc, g + 1)
                dve.wait_ge(delta_ps, g)
                dve.wait_ge(ctx_ps, g)

                def fl(x):
                    return x[:, :, :].rearrange("p i t -> p (i t)")
                dve.tensor_tensor_scan(fl(cumT), fl(first0), fl(xc), 0.0, ALU.mult, ALU.add).then_inc(scan_step, 1)
                dve.tensor_tensor_scan(fl(ctxT), fl(decay), fl(xc), 0.0, ALU.mult, ALU.add).then_inc(ctx_ready, 1)

            def c1_diff(g, h, j):
                dve.wait_ge(scan_step, g + 1)
                dve.tensor_tensor(cumT[:, :, 1:], cumT[:, :, 1:], xc[:, :, 0:SEQ - 1], ALU.subtract)\
                    .then_inc(delta_ready, 1)

            scan_step = sem("scan_step")

            def c2(g, h, j):
                s = S["L1"]
                dve.wait_ge(actx_ready, g + 1)
                dve.wait_ge(s.resid_out[h], 16 * j)
                dve.tensor_tensor(htok[h][:, :, :], h2tok[h][:, :, :], actx[:, :, :], ALU.add)\
                    .then_inc(s.htok_ready, 1)

            def mid_step(g, h, j, ahead, ahead2=True):
                o, jo = 1 - h, j + h
                if ahead:
                    c0_apply(g + 1, o, jo)
                r1(L1, g, h, j)
                if ahead:
                    c1(g + 1, o, jo)
                r1_apply(L1, g, h, j)
                if ahead:
                    c1_diff(g + 1, o, jo)
                if ahead2:
                    c0(g + 2, h, j + 1)
                st = r2(L1, g, h, j)
                r3(L1, g, h, j, st)
                if ahead:
                    c2(g + 1, o, jo)
                assert st.n + 1 == NR["L1"], st.n

            ins = dve.memset(seen[:, :], 0.0)
            ins.then_inc(consts_dve, 1)
            dve.wait_ge(exp_ready, GROUPS + 1)
            dve.tensor_scalar(kcol[:, 1:2], kcol[:, 1:2], 1.0, None, ALU.add).then_inc(consts_dve, 1)
            dve.wait_ge(consts_dve, 3)
            dve.reciprocal(kcol[:, 1:2], kcol[:, 1:2]).then_inc(consts_dve, 1)
            dve.wait_ge(consts_dve, 4)
            dve.tensor_scalar(decay[:, :, :], first0[:, :, :], kcol[:, 1:2], None, ALU.mult)\
                .then_inc(consts_dve, 1)
            dve.wait_ge(consts_dve, 5)
            for f in (c0, c0_apply, c1, c1_diff):
                f(0, 0, 0)
            c0(1, 1, 0)
            c2(0, 0, 0)
            for h in range(2):
                mid_step(h, h, 0, True)
            with dve.Fori(1, GROUPS // 2 - 1) as j:
                for h in range(2):
                    mid_step(2 * j + h, h, j, True)
            j = GROUPS // 2 - 1
            mid_step(2 * j, 0, j, True, False)
            mid_step(2 * j + 1, 1, j, False, False)
            tables(L1)
            expert_blocks(L1)
            def total(g, h, j):
                dve.wait_ge(e_in[h], 32 * (j + 1))
                dve.wait_ge(e_out[h], 16 * j)
                dve.tensor_tensor(fin[h][:, :, :], yin[h][:, :, 0, :], yin[h][:, :, 1, :], ALU.add)\
                    .then_inc(e_dve, 1)
                dve.wait_ge(e_dve, g + 1)
                dve.tensor_tensor(fin[h][:, :, :], fin[h][:, :, :], hin[h][:, :, :], ALU.add)\
                    .then_inc(e_ready, 1)
            pairs(dve, total)

        @block.gpsimd
        def _(pool):
            n = [0]

            def link(ins):
                n[0] += 1
                ins.then_inc(made_step, 1)
                pool.wait_ge(made_step, n[0])

            def fill(t, value, keep, base, pattern, mult):
                link(pool.affine_select(out=t, in_=t, compare_op=keep, fill=value, base=base, pattern=pattern,
                                        channel_multiplier=mult))
            link(pool.memset(ident[:, :], 0.0))
            fill(ident[:, :], 1.0, ALU.not_equal, 0, [[-1, 128]], 1)
            link(pool.memset(ones[:, :], 1.0))
            link(pool.memset(ones16[:, :], 1.0))
            link(pool.memset(before16[:, :], 1.0))
            fill(before16[:, :], 0.0, ALU.is_gt, 0, [[1, 128]], -1)
            link(pool.memset(upto[:, :], 1.0))
            fill(upto[:, :], 0.0, ALU.is_ge, 0, [[1, 32]], -1)
            link(pool.memset(causal[:, :], 0.0))
            fill(causal[:, :], MASKED, ALU.is_ge, 0, [[1, SEQ]], -1)
            link(pool.iota(iotaE[:, :], pattern=[[1, 32]], base=0, channel_multiplier=0,
                           allow_small_or_imprecise_dtypes=True))
            link(pool.iota(iotaB[:, :], pattern=[[1, 192]], base=0, channel_multiplier=0,
                           allow_small_or_imprecise_dtypes=True))
            link(pool.iota(place0[:, :, :], pattern=[[TOP * ROWS, TILES], [1, TOP]], base=0,
                           channel_multiplier=TOP, allow_small_or_imprecise_dtypes=True))
            link(pool.tensor_copy(place[:, :, :], place0[:, :, :]))
            link(pool.memset(half_m[:, :], -0.5))
            link(pool.memset(half_p[:, :], 0.5))
            link(pool.memset(seen[:, :], 0.0))
            link(pool.memset(padrows[:, :, :], 0.0))
            link(pool.memset(padrows[:, :, PLACE:PLACE + 1].bitcast(I32), NOWHERE))
            for h in range(2):
                link(pool.memset(rows[h][:, :, :, D:ROW], 0.0))
                link(pool.memset(h0T[h][:, :, 0:1], 0.0))
            link(pool.memset(first0[:, :, :], 1.0))
            pool.memset(first0[:, :, 0:1], 0.0).then_inc(made, 1)
            last = pool.to_reg(TOKENS * TOP - 1)

            def rstd(ln, g, stats, ready, steps):
                pool.wait_ge(stats, g + 1)
                past(pool, pool_passed)
                pool.tensor_scalar(ln.ve[:, :], ln.mv[:, :, 1], EPS, None, ALU.add).then_inc(steps, 1)
                pool.wait_ge(steps, g + 1)
                pool.tensor_tensor(ln.rs[:, :], ln.ve[:, :], half_m[0:ROWS, :], ALU.pow).then_inc(ready, 1)

            def r1(l, g, h, j):
                s = S[l.name]
                rstd(LNB, g, s.statsB, s.rstdB, s.poolR)

            def places(l, g, h, j):
                s = S[l.name]
                pool.wait_ge(s.scattered[h], 16 * TILES * TOP * j)
                past(pool, pool_passed)
                pool.tensor_copy(rows[h][:, :, :, PLACE].bitcast(I32), place[:, :, :]).then_inc(s.place_ready, 1)
                pool.wait_ge(s.place_ready, 2 * g + 1)
                past(pool, pool_passed)
                pool.tensor_scalar(place[:, :, :], place[:, :, :], float(TOP * GT), None, ALU.add)\
                    .then_inc(s.place_ready, 1)

            def send(l, g, h):
                s = S[l.name]
                pool.wait_ge(s.rows1_ready, g + 1)
                pool.wait_ge(s.gate_ready, g + 1)
                pool.wait_ge(s.slot_ready, g + 1)
                pool.wait_ge(s.place_ready, 2 * g + 2)
                past(pool, pool_passed)
                for t in range(TILES):
                    for k in range(TOP):
                        pool.indirect_dma_start(
                            out=lists[l.name], out_offset=bass.IndirectOffsetOnAxis(ap=slots[h][:, t, k:k + 1], axis=0),
                            in_=rows[h][:, t, k, :], in_offset=None).then_inc(s.scattered[h], 16)

            def front_step(g, h, j, ahead):
                if ahead:
                    rstd(LNA, g + 1, statsA, rstdA, poolA)
                r1(L0, g, h, j)
                places(L0, g, h, j)
                if not (isinstance(g, int) and g == 0):
                    send(L0, g - 1, 1 - h)

            rstd(LNA, 0, statsA, rstdA, poolA)
            for h in range(2):
                front_step(h, h, 0, True)
            with pool.Fori(1, GROUPS // 2 - 1) as j:
                for h in range(2):
                    front_step(2 * j + h, h, j, True)
            j = GROUPS // 2 - 1
            front_step(2 * j, 0, j, True)
            front_step(2 * j + 1, 1, j, False)
            send(L0, GROUPS - 1, 1)

            def expert_blocks(l):
                k = K[l.name]
                def send_results(u, j):
                    pool.wait_ge(k.y_ready, k.i0 + l.unroll * j + u + 1)
                    pool.wait_ge(k.blk_in[u], 32 * (k.j0 + j + 1))
                    past(pool, pool_passed)
                    for q in range(l.Q):
                        pool.indirect_dma_start(
                            out=results[l.name], out_offset=bass.IndirectOffsetOnAxis(
                                ap=xblk[u][:, q, PLACE:PLACE + 1].bitcast(U32), axis=0),
                            in_=yblk[u][:, q, :], in_offset=None, bounds_check=last, oob_is_err=False)\
                            .then_inc(k.y_out[u], 16)

                rounds(pool, l, send_results)

            expert_blocks(L0)

            def mid_a(g):
                rstd(LNA, g, m_statsA, m_rstdA, poolM)

            def mid_b(g):
                pool.wait_ge(ssq_ready, g + 1)
                pool.wait_ge(actx_ready, g)
                pool.tensor_tensor(mag[:, :], ssq[:, :], half_p[0:ROWS, :], ALU.pow).then_inc(mag_ready, 1)

            def mid_step(g, h, j, ahead, ahead2=True):
                r1(L1, g, h, j)
                if ahead2:
                    mid_a(g + 2)
                if ahead:
                    mid_b(g + 1)
                places(L1, g, h, j)
                if not (isinstance(g, int) and g == 0):
                    send(L1, g - 1, 1 - h)

            for h in range(2):
                pool.wait_ge(S["L0"].scattered[h], 16 * TILES * TOP * GROUPS // 2)
            pool.tensor_copy(place[:, :, :], place0[:, :, :]).then_inc(made_step, 1)
            n[0] += 1
            pool.wait_ge(made_step, n[0])
            mid_a(0)
            mid_a(1)
            mid_b(0)
            for h in range(2):
                mid_step(h, h, 0, True)
            with pool.Fori(1, GROUPS // 2 - 1) as j:
                for h in range(2):
                    mid_step(2 * j + h, h, j, True)
            j = GROUPS // 2 - 1
            mid_step(2 * j, 0, j, True, False)
            mid_step(2 * j + 1, 1, j, False, False)
            send(L1, GROUPS - 1, 1)
            expert_blocks(L1)


def laid_out(v):
    import numpy as np
    f = {k: np.asarray(x) for k, x in v.items()}
    x = f["x"].reshape(GROUPS, GI, 3, 8, 28, 8, 28).transpose(0, 2, 4, 6, 1, 3, 5).reshape(GROUPS, IN_D, GP)
    main = x[:, :KT * 128].reshape(GROUPS, CHUNKS, KC, 128, GP).transpose(0, 1, 3, 2, 4)
    wT = f["L0_tok_W"].T
    w1 = f["L1_ffn_w1"].transpose(0, 2, 1)
    w2 = f["L1_ffn_w2"].transpose(0, 2, 1).reshape(L1.E, L1.FC, 128, D).transpose(0, 2, 1, 3)
    b1 = f["L1_ffn_b1"].reshape(L1.E, L1.FC, 128).transpose(0, 2, 1)
    b2 = np.broadcast_to(f["L1_ffn_b2"][:, None, :], (L1.E, 128, D))
    a = {
        "x_main": main.reshape(GROUPS * CHUNKS, 128, KC * GP),
        "x_rest": x[:, KT * 128:],
        "w_main": wT[:KT * 128].reshape(KT, 128, D).transpose(1, 0, 2).reshape(128, KT * D),
        "w_rest": wT[KT * 128:],
        "wq": f["L0_attn_Wq"], "wk": f["L0_attn_Wk"], "wv": f["L0_attn_Wv"],
        "cols": np.stack([f["L0_tok_b"], f["L0_attn_bq"], f["L0_attn_bk"], f["L0_tok_class_token"][0]], 1),
        "bv": f["L0_attn_bv"][None, :],
        "posT": f["L0_tok_pos_embed"].T,
        "selT0": f["L0_ffn_expert_sel"].T,
        "selT1": f["L1_ffn_router_w"].T,
        "rb": f["L1_ffn_router_b"][None, :],
        "k": f["L1_attn_k"].reshape(1, 1),
        "w_L0": np.concatenate([f["L0_ffn_keys"], f["L0_ffn_values"]], 2).reshape(L0.E * 128, L0.W),
        "w_L1": np.concatenate([w1, w2.reshape(L1.E, 128, L1.FC * D), b1, b2], 2).reshape(L1.E * 128, L1.W),
    }
    return {k: np.ascontiguousarray(x) for k, x in a.items()}


def kernel(**inputs):
    import concourse.bacc as bacc
    from concourse.bass_utils import run_bass_kernel_spmd
    arrays = laid_out(inputs)
    nc = bacc.Bacc("TRN2", target_bir_lowering=False, num_devices=1)
    a = {n: nc.dram_tensor(f"in_{n}", x.shape, mybir.dt.from_np(x.dtype), kind="ExternalInput").ap()
         for n, x in arrays.items()}
    out = nc.dram_tensor("out_0", (TOKENS, D), F32, kind="ExternalOutput").ap()
    build(nc, a, out)
    r = run_bass_kernel_spmd(nc, [{f"in_{n}": x for n, x in arrays.items()}], core_ids=[0])
    return r.results[0]["out_0"].reshape(IMAGES, SEQ, D)
```

```python
from contextlib import ExitStack

import concourse.bass as bass
from concourse import mybir

F32 = mybir.dt.float32
F32R = mybir.dt.float32r
BF16 = mybir.dt.bfloat16
U32 = mybir.dt.uint32
I32 = mybir.dt.int32
ALU = mybir.AluOpType
ACT = mybir.ActivationFunctionType
X = mybir.AxisListType.X

IMAGES, SEQ, D = 128, 65, 128
PATCHES = SEQ - 1
TOKENS = IMAGES * SEQ
GROUPS = 16
NE = 4
GI = IMAGES // GROUPS
GT = GI * SEQ
GP = GI * PATCHES
TILES = 5
ROWS = GT // TILES
HALF = GT // 2
TOP = 2
IN_D = 3 * 28 * 28
KT = IN_D // 128
KREST = IN_D - KT * 128
CHUNKS = 3
KC = KT // CHUNKS
SPLIT = CHUNKS - 1
BANK = 512
EPS = 1e-5
MASKED = -1e30
ROW = D + 4
PLACE, GATE = D, D + 1
NOWHERE = TOKENS * TOP
NB = 8


class Layer:

    def __init__(self, turn, name, experts, hidden, block, unroll=NB):
        self.turn = turn
        self.name, self.E, self.FC, self.block = name, experts, hidden // 128, block
        self.Q = block // 128
        self.shift = block.bit_length() - 1
        self.room = TOKENS + block
        self.step = experts * self.room + 1
        most = (TOKENS * TOP + experts * (block - 1)) // block
        self.unroll = unroll
        self.blocks = -(-most // unroll) * unroll
        self.W = 2 * hidden + (self.FC + D if self.FC > 1 else 0)


L0 = Layer(1, "L0", 32, 128, 256)
L1 = Layer(2, "L1", 16, 512, 256)
SMALL = 3 * D + SEQ + L0.E + L1.E + 4


def past(eng, passed):
    eng.sem_inc(passed, 1)


class Steps:

    def __init__(self, base):
        self.base, self.n = base, 0

    def one(self):
        self.n += 1
        return 1

    def all(self):
        return self.base + self.n


class Norm:

    def __init__(self, sb, n):
        self.bn, self.mv = sb(f"bn{n}", [ROWS, TILES, 6]), sb(f"mv{n}", [ROWS, TILES, 2])
        self.ve, self.rs = sb(f"ve{n}", [ROWS, TILES]), sb(f"rs{n}", [ROWS, TILES])


class Tables:

    def __init__(self, sb):
        self.cnt, self.up, self.nb = sb("t_cnt", [32, 1]), sb("t_up", [32, 1], I32), sb("t_nb", [32, 1])
        self.cb, self.ge, self.v = sb("t_cb", [32, 1]), sb("t_ge", [32, 192]), sb("t_v", [32, 2])
        self.ef, self.rf = sb("t_ef", [1, 192]), sb("t_rf", [1, 192])
        self.entry = sb("t_entry", [1, 192], I32)
        self.fr = sb("t_fr", [1, 32], I32)


class TableSignals:

    def __init__(self, sem):
        self.cnt_ps = sem("cnt_ps")
        self.nb_ready = sem("nb_ready")
        self.cb_ps = sem("cb_ps")
        self.ge_ready = sem("ge_ready")
        self.tab_ps = sem("tab_ps")
        self.tables_ready = sem("tables_ready")
        self.fr_ready = sem("fr_ready")
        self.pads_in = sem("pads_in")
        self.table_step = sem("table_step")


class LayerSignals:

    def __init__(self, sem, halves, n):
        self.htok_ready = sem(f"{n}_htok_ready")
        self.statsB = sem(f"{n}_statsB")
        self.rstdB = sem(f"{n}_rstdB")
        self.rows0_ready = sem(f"{n}_rows0_ready")
        self.rows1_ready = sem(f"{n}_rows1_ready")
        self.x2T_ps = sem(f"{n}_x2T_ps")
        self.x2T_ready = sem(f"{n}_x2T_ready")
        self.lg_ps = sem(f"{n}_lg_ps")
        self.top_ready = sem(f"{n}_top_ready")
        self.oh_ready = sem(f"{n}_oh_ready")
        self.rank_ps = sem(f"{n}_rank_ps")
        self.rank_read = sem(f"{n}_rank_read")
        self.slot_ready = sem(f"{n}_slot_ready")
        self.eg_ready = sem(f"{n}_eg_ready")
        self.gate_ready = sem(f"{n}_gate_ready")
        self.place_ready = sem(f"{n}_place_ready")
        self.dveR = sem(f"{n}_dveR")
        self.poolR = sem(f"{n}_poolR")
        self.scattered = halves(f"{n}_scattered")
        self.resid_out = halves(f"{n}_resid_out")


class BlockSignals:

    def __init__(self, sem, i0, j0, y0, first=None):
        self.i0, self.j0, self.y0 = i0, j0, y0
        if first is None:
            self.blk_in = [sem(f"blk_in{u}") for u in range(NB)]
            self.y_out = [sem(f"y_out{u}") for u in range(NB)]
            self.xT_ps, self.xT_ready = sem("bxT_ps"), sem("bxT_ready")
            self.h_ps, self.h_ready = sem("bh_ps"), sem("bh_ready")
            self.y_ps, self.y_ready = sem("by_ps"), sem("by_ready")
        else:
            self.blk_in, self.y_out = first.blk_in, first.y_out
            self.xT_ps, self.xT_ready = first.xT_ps, first.xT_ready
            self.h_ps, self.h_ready = first.h_ps, first.h_ready
            self.y_ps, self.y_ready = first.y_ps, first.y_ready


def build(nc, a, out):
    ctx = ExitStack()
    with ctx:
        def sb(name, shape, dt=F32):
            return ctx.enter_context(nc.sbuf_tensor(name, shape, dt))

        def part(tensor, p, at, n):
            return tensor[0:p, :, :].rearrange("p a b -> p (a b)")[:, at:at + n]

        def sem(name):
            return ctx.enter_context(nc.semaphore(name))

        def halves(name):
            return [sem(f"{name}{h}") for h in range(2)]

        def dram(name, shape):
            return nc.dram_tensor(name, shape, F32, kind="Internal").ap()

        lists = {l.name: dram(f"lists_{l.name}", [l.E * l.room + l.block, ROW]) for l in (L0, L1)}
        results = {l.name: dram(f"results_{l.name}", [TOKENS * TOP, D]) for l in (L0, L1)}
        resid = {l.name: dram(f"resid_{l.name}", [GROUPS, ROWS, TILES * D]) for l in (L0, L1)}

        ps = ctx.enter_context(nc.psum_tensor("ps", [128, 8, BANK], F32))
        psE = [ps[:, h, :] for h in range(2)]
        pair = [ps[:, 2 + 2 * n:4 + 2 * n, :].rearrange("p b n -> p (b n)") for n in range(3)]

        ident = sb("ident", [128, 128])
        w_emb = sb("w_emb", [128, KT, D])
        w_hi, w_lo = sb("w_hi", [128, KC, D], F32R), sb("w_lo", [128, KC, D], F32R)
        w_rest = sb("w_rest", [KREST, D])
        small = sb("small", [D, SMALL])
        wq, wk, wv = (small[:, n * D:(n + 1) * D] for n in range(3))
        posT = small[:, 3 * D:3 * D + SEQ]
        selT = {"L0": small[:, 3 * D + SEQ:][:, 0:L0.E], "L1": small[:, 3 * D + SEQ + L0.E:][:, 0:L1.E]}
        cols = small[:, SMALL - 4:SMALL]
        per_row = sb("per_row", [128, D + L1.E + 1])
        bv_rows = per_row[0:SEQ, 0:D]
        rb_rows = per_row[0:ROWS, D:D + L1.E]
        causal = sb("causal", [SEQ, SEQ])
        ones = sb("ones", [128, 128])
        ones16 = sb("ones16", [128, 128], BF16)
        before16 = sb("before16", [128, 128], BF16)
        upto = sb("upto", [32, 32])
        iotaE = sb("iotaE", [ROWS, 32])
        iotaB = sb("iotaB", [32, 192])
        half_m = sb("half_m", [128, TILES])
        half_p = sb("half_p", [128, TILES])
        place0 = sb("place0", [ROWS, TILES, TOP])
        padrows = sb("padrows", [128, 2, ROW])
        kcol = sb("kcol", [128, 2])
        first0 = sb("first0", [128, GI, SEQ])
        decay = sb("decay", [128, GI, SEQ])

        xin = [[sb(f"xin{h}_{c}", [128, KC, GP]) for c in range(CHUNKS)] for h in range(2)]
        x_hi, x_lo = sb("x_hi", [128, KC, GP], F32R), sb("x_lo", [128, KC, GP], F32R)
        xrest = [sb(f"xrest{h}", [KREST, GP]) for h in range(2)]
        h0T = [sb(f"h0T{h}", [D, GI, SEQ]) for h in range(2)]
        x1T = [sb(f"x1T{h}", [D, GT]) for h in range(2)]
        QT, KTt = sb("QT", [D, GT]), sb("KT", [D, GT])
        V = [sb(f"V{h}", [SEQ, GI, D]) for h in range(2)]
        Sm = sb("Sm", [SEQ, GI, SEQ])
        Pr = [sb(f"Pr{h}", [SEQ, GI, SEQ]) for h in range(2)]
        smax = sb("smax", [SEQ, GI])
        ssum = sb("ssum", [SEQ, GI])
        u0T = sb("u0T", [D, GT])
        h1T = sb("h1T", [D, GT])
        atok = sb("atok", [ROWS, TILES, D])
        ntok = sb("ntok", [ROWS, TILES, D])
        LNA, LNB = Norm(sb, "A"), Norm(sb, "B")
        htok = [sb(f"htok{h}", [ROWS, TILES, D]) for h in range(2)]
        rows = [sb(f"rows{h}", [ROWS, TILES, TOP, ROW]) for h in range(2)]
        x2T = sb("x2T", [D, TILES, ROWS])
        lg = sb("lg", [ROWS, TILES, 32])
        top8 = sb("top8", [ROWS, TILES, 8])
        idx8 = sb("idx8", [ROWS, TILES, 8], U32)
        chosen = sb("chosen", [ROWS, TILES, TOP])
        oh = sb("oh", [ROWS, TILES, TOP, 32], BF16)
        ohs = sb("ohs", [ROWS, TILES, 32], BF16)
        seen = sb("seen", [ROWS, 32], BF16)
        added = sb("added", [ROWS, 32])
        pick = sb("pick", [ROWS, TILES, TOP, 32])
        rank = sb("rank", [ROWS, TILES, TOP])
        slots = [sb(f"slots{h}", [ROWS, TILES, TOP], U32) for h in range(2)]
        eg = sb("eg", [ROWS, TILES, TOP])
        gsum = sb("gsum", [ROWS, TILES])
        lgs = sb("lgs", [ROWS, TILES, 32])
        place = sb("place", [ROWS, TILES, TOP])
        tb = Tables(sb)
        wblk = [part(xin[u % 2][u // 4], 128, u // 2 % 2 * L1.W, L1.W) for u in range(NB)]
        xblk = [part(xin[u % 2][2], 128, u // 2 * 2 * ROW, 2 * ROW).rearrange("p (q w) -> p q w", q=2)
                for u in range(NB)]
        yblk = [part(xin[u % 2][2], 128, 8 * ROW + u // 2 * 2 * D, 2 * D).rearrange("p (q d) -> p q d", q=2)
                for u in range(NB)]
        xTb = [sb(f"xTb{h}", [D, 2 * 128]) for h in range(2)]
        w1hi, w1lo = ([part(x, 128, h * 512, 512) for h in range(2)] for x in (x_hi, x_lo))
        xbhi, xblo = ([part(x, 128, 1024 + h * 256, 256) for h in range(2)] for x in (x_hi, x_lo))
        hTb = [sb(f"hTb{h}", [128, 4, 256]) for h in range(2)]
        yin = [part(xin[h][1], ROWS, 0, TILES * TOP * D).rearrange("p (t k d) -> p t k d", t=TILES, k=TOP)
               for h in range(2)]
        h2tok, hin = ([part(xin[h][1], ROWS, n * TILES * D, TILES * D).rearrange("p (t d) -> p t d", t=TILES)
                       for h in range(2)] for n in (2, 3))
        ends = [xin[u % 2][u // 2] for u in range(NE)]
        end_y = [part(x, ROWS, 0, TILES * TOP * D).rearrange("p (t k d) -> p t k d", t=TILES, k=TOP) for x in ends]
        end_h, fin = ([part(x, ROWS, n * TILES * D, TILES * D).rearrange("p (t d) -> p t d", t=TILES)
                       for x in ends] for n in (2, 3))
        actx, sq = (part(xin[1][2], ROWS, n * TILES * D, TILES * D).rearrange("p (t d) -> p t d", t=TILES)
                    for n in (2, 3))
        cumT, ctxT = (part(xin[h][2], D, TILES * D, GT).rearrange("p (i t) -> p i t", i=GI) for h in range(2))
        xc = part(xin[0][2], D, 2 * TILES * D, GT).rearrange("p (i t) -> p i t", i=GI)
        ssq = sb("ssq", [ROWS, TILES])
        mag = sb("mag", [ROWS, TILES])

        w_emb_in = sem("w_emb_in")
        w_rest_in = sem("w_rest_in")
        w_hi_ready = sem("w_hi_ready")
        x_hi_ready = sem("x_hi_ready")
        split = sem("split")
        consts_in = sem("consts_in")
        made = sem("made")
        made_step = sem("made_step")
        consts_dve = sem("consts_dve")
        chunk_in = [[sem(f"chunk_in{h}_{c}") for c in range(CHUNKS)] for h in range(2)]
        chunk_used = [[sem(f"chunk_used{h}_{c}") for c in range(CHUNKS)] for h in range(2)]
        emb_ps = sem("emb_ps")
        h0T_ready = sem("h0T_ready")
        h0_ps = sem("h0_ps")
        atok_ready = sem("atok_ready")
        statsA = sem("statsA")
        rstdA = sem("rstdA")
        ntok_ready = sem("ntok_ready")
        xT_ps = sem("xT_ps")
        x1T_ready = sem("x1T_ready")
        q_ps, k_ps, v_ps, s_ps = sem("q_ps"), sem("k_ps"), sem("v_ps"), sem("s_ps")
        q_ready, k_ready, v_ready = sem("q_ready"), sem("k_ready"), sem("v_ready")
        s_read = sem("s_read")
        shifted = sem("shifted")
        exp_ready = sem("exp_ready")
        p_ready = sem("p_ready")
        read_ps = sem("read_ps")
        h1T_ready = sem("h1T_ready")
        hT_ps = sem("hT_ps")
        dveA = sem("dveA")
        dveB = sem("dveB")
        poolA = sem("poolA")

        T = TableSignals(sem)
        S = {l.name: LayerSignals(sem, halves, l.name) for l in (L0, L1)}
        K = {"L0": BlockSignals(sem, 0, 0, 0)}
        K["L1"] = BlockSignals(sem, L0.blocks, L0.blocks // NB, 16 * L0.Q * L0.blocks // NB, K["L0"])
        m_in = halves("m_in")
        m_free = halves("m_free")
        m_statsA, m_rstdA, m_ntok, m_xT_ps, m_xc = (sem(n) for n in (
            "m_statsA", "m_rstdA", "m_ntok", "m_xT_ps", "m_xc"))
        ctx_ready, delta_ready, ctx_ps, delta_ps, ssq_ready, mag_ready, actx_ready = (sem(n) for n in (
            "ctx_ready", "delta_ready", "ctx_ps", "delta_ps", "ssq_ready", "mag_ready", "actx_ready"))
        dveM, poolM = sem("dveM"), sem("poolM")
        dve_passed, pool_passed = sem("dve_passed"), sem("pool_passed")
        y_biased = sem("y_biased")
        w1hi_ready = sem("w1hi_ready")
        xhi_ready = sem("xhi_ready")
        e_in = [sem(f"e_in{u}") for u in range(NE)]
        e_ready = sem("e_ready")
        e_dve = sem("e_dve")
        e_out = [sem(f"e_out{u}") for u in range(NE)]

        block = ctx.enter_context(nc.Block())

        def pairs(eng, body, n=GROUPS):
            for h in range(2):
                body(h, h, 0)
            with eng.Fori(1, n // 2) as j:
                for h in range(2):
                    body(2 * j + h, h, j)

        def ring(eng, body):
            for u in range(NE):
                body(u, u, 0)
            with eng.Fori(1, GROUPS // NE) as j:
                for u in range(NE):
                    body(NE * j + u, u, j)

        NCONST = 2

        def rounds(eng, l, body):
            for u in range(l.unroll):
                body(u, 0)
            with eng.Fori(1, l.blocks // l.unroll) as j:
                for u in range(l.unroll):
                    body(u, j)

        def pads(eng, l, half):
            pad = padrows[:, 0:l.Q, :].rearrange("p q w -> p (q w)")
            room = lists[l.name]
            eng.wait_ge(made, 1)
            if half == 0:
                eng.dma_start(room[l.E * l.room:, :].rearrange("(p q) w -> p (q w)", q=l.Q), pad)\
                    .then_inc(T.pads_in, 16)
            eng.wait_ge(T.fr_ready, l.turn)
            with eng.Fori(0, l.E // 8) as e:
                for u in range(4):
                    at = eng.value_load(tb.fr[0:1, bass.ds(half * (l.E // 2) + 4 * e + u, 1)], min_val=0,
                                        max_val=l.E * l.room - l.block)
                    eng.dma_start(room[bass.ds(at, l.block), :].rearrange("(p q) w -> p (q w)", q=l.Q), pad)\
                        .then_inc(T.pads_in, 16)

        def sp_blocks(sp, l):
            s, k = S[l.name], K[l.name]
            room = lists[l.name]
            pads(sp, l, 0)
            sp.wait_ge(T.tables_ready, l.turn)
            sp.wait_ge(T.pads_in, 16 * (l.E + 1) + (16 * (L0.E + 1) if l is L1 else 0))
            for h in range(2):
                sp.wait_ge(s.scattered[h], 16 * TILES * TOP * GROUPS // 2)
            weights = a[f"w_{l.name}"]

            def load(u, j):
                i = l.unroll * j + u
                entry = sp.value_load(tb.entry[0:1, bass.ds(i, 1)], min_val=0, max_val=l.E * l.step - 1)
                e, r = entry // l.step, entry % l.step
                sp.wait_ge(k.y_out[u], k.y0 + 16 * l.Q * j)
                sp.dma_start(wblk[u][:, 0:l.W], weights[bass.ds(e * 128, 128), :]).then_inc(k.blk_in[u], 16)
                sp.dma_start(xblk[u][:, 0:l.Q, :].rearrange("p q w -> p (q w)"),
                             room[bass.ds(r, l.block), :].rearrange("(p q) w -> p (q w)", q=l.Q))\
                    .then_inc(k.blk_in[u], 16)

            rounds(sp, l, load)

        def sp_group_in(sp, name, g, h, y_in, h_in, got):
            sp.dma_start(y_in[h].rearrange("p t k d -> p t (k d)"),
                         results[name].rearrange("(g t p k) d -> g p t (k d)", g=GROUPS, p=ROWS, t=TILES)[
                             bass.ds(g, 1), :, :, :].rearrange("o p t n -> (o p) t n")).then_inc(got, 16)
            sp.dma_start(h_in[h][:, :, :].rearrange("p t d -> p (t d)"),
                         resid[name][bass.ds(g, 1), :, :].rearrange("o p n -> (o p) n")).then_inc(got, 16)

        @block.sync
        def _(sp):
            def load_patches(g, h, j):
                for c in range(CHUNKS):
                    sp.wait_ge(chunk_used[h][c], j)
                    sp.dma_start(xin[h][c][:, :, :].rearrange("p k n -> p (k n)"),
                                 a["x_main"][bass.ds(g * CHUNKS + c, 1), :, :].rearrange("o p n -> (o p) n"))\
                        .then_inc(chunk_in[h][c], 16)
                    if c == CHUNKS - 1:
                        sp.dma_start(xrest[h][:, :], a["x_rest"][bass.ds(g, 1), :, :]
                                     .rearrange("o p n -> (o p) n")).then_inc(chunk_in[h][c], 16)
            pairs(sp, load_patches)
            sp_blocks(sp, L0)
            for u in range(NB):
                sp.wait_ge(K["L0"].y_out[u], 16 * L0.Q * L0.blocks // L0.unroll)
            for h in range(2):
                sp.wait_ge(S["L0"].resid_out[h], 16 * GROUPS // 2)

            def load_mid(g, h, j):
                sp.wait_ge(m_free[h], j)
                sp_group_in(sp, "L0", g, h, yin, hin, m_in[h])
            pairs(sp, load_mid)
            sp_blocks(sp, L1)
            for u in range(NB):
                sp.wait_ge(K["L1"].y_out[u], K["L1"].y0 + 16 * L1.Q * L1.blocks // L1.unroll)
            for h in range(2):
                sp.wait_ge(S["L1"].resid_out[h], 16 * GROUPS // 2)

            def load_end(g, u, j):
                if not isinstance(j, int):
                    sp.wait_ge(e_ready, NE * (j - 1) + u + 1)
                sp_group_in(sp, "L1", g, u, end_y, end_h, e_in[u])
            ring(sp, load_end)

        @block.tensor
        def _(pe):
            pe.wait_ge(w_emb_in, 16)

            def embed(g, h, j, first, end):
                for k in range(first, end):
                    c, n = divmod(k, KC)
                    if n == 0:
                        pe.wait_ge(chunk_in[h][c], (j + 1) * (32 if c == CHUNKS - 1 else 16))
                        if c == SPLIT:
                            pe.wait_ge(split, g + 2)
                    if c == SPLIT:
                        for w, x in ((w_lo, x_hi), (w_hi, x_lo), (w_hi, x_hi)):
                            mm = pe.matmul(psE[h], w[:, n, :], x[:, n, :], start=False, stop=False,
                                           skip_group_check=True)
                    else:
                        mm = pe.matmul(psE[h], w_emb[:, k, :], xin[h][c][:, n, :], start=(k == 0), stop=False,
                                       skip_group_check=True)
                    if k == KT - 1:
                        mm = pe.matmul(psE[h], w_rest[:, :], xrest[h][:, :], start=False, stop=True,
                                       skip_group_check=True)
                    if n == KC - 1:
                        mm.then_inc(chunk_used[h][c], 1)

            def tok_from_T(srcT, p):
                for t in range(TILES):
                    mm = pe.transpose(pair[p][0:ROWS, t * 128:(t + 1) * 128], srcT[:, t * ROWS:(t + 1) * ROWS],
                                      ident[:, :])
                return mm

            def T_from_tok(tile, p):
                for t in range(TILES):
                    mm = pe.transpose(pair[p][:, t * 128:t * 128 + ROWS], tile(t), ident[0:ROWS, 0:ROWS])
                return mm

            def a1(g, h, j):
                pe.wait_ge(h0T_ready, g + 1)
                pe.wait_ge(v_ready, g)
                tok_from_T(h0T[h][:, :, :].rearrange("p i t -> p (i t)"), 0).then_inc(h0_ps, 1)

            def a2(g, h, j):
                pe.wait_ge(ntok_ready, g + 1)
                T_from_tok(lambda t: ntok[:, t, :], 0).then_inc(xT_ps, 1)

            def a3(g, h, j):
                pe.wait_ge(x1T_ready, g + 1)
                for n in range(2):
                    mm = pe.matmul(pair[0][:, n * BANK:n * BANK + HALF], wq[:, :], x1T[h][:, n * HALF:(n + 1) * HALF],
                                   start=True, stop=True)
                mm.then_inc(q_ps, 1)
                pe.wait_ge(s_read, g)
                for n in range(2):
                    mm = pe.matmul(pair[1][:, n * BANK:n * BANK + HALF], wk[:, :], x1T[h][:, n * HALF:(n + 1) * HALF],
                                   start=True, stop=True)
                mm.then_inc(k_ps, 1)

            def a4(g, h, j):
                pe.wait_ge(q_ready, g + 1)
                for i in range(GI):
                    mm = pe.matmul(pair[0][0:SEQ, i * D:(i + 1) * D], x1T[h][:, i * SEQ:(i + 1) * SEQ], wv[:, :],
                                   start=True, stop=True)
                mm.then_inc(v_ps, 1)
                pe.wait_ge(k_ready, g + 1)
                for i in range(GI):
                    c = i // 4 * BANK + i % 4 * SEQ
                    mm = pe.matmul(pair[1][0:SEQ, c:c + SEQ], KTt[:, i * SEQ:(i + 1) * SEQ],
                                   QT[:, i * SEQ:(i + 1) * SEQ], start=True, stop=True)
                mm.then_inc(s_ps, 1)

            def b1(g, h, j):
                pe.wait_ge(p_ready, g + 1)
                pe.wait_ge(v_ready, g + 1)
                pe.wait_ge(S["L0"].rank_read, g)
                for i in range(GI):
                    c = i // 4 * BANK + i % 4 * SEQ
                    mm = pe.matmul(pair[2][:, c:c + SEQ], V[h][:, i, :], Pr[h][:, i, :], start=True, stop=True)
                mm.then_inc(read_ps, 1)

            def b2(g, h, j):
                pe.wait_ge(h1T_ready, g + 1)
                tok_from_T(h1T[:, :], 2).then_inc(hT_ps, 1)

            def r1(l, g, h, j):
                s = S[l.name]
                pe.wait_ge(s.rows0_ready, g + 1)
                if l is L1:
                    pe.wait_ge(s.rank_read, g)
                T_from_tok(lambda t: rows[h][:, t, 0, 0:D], 2).then_inc(s.x2T_ps, 1)

            def r2(l, g, h, j):
                s = S[l.name]
                pe.wait_ge(s.x2T_ready, g + 1)
                for t in range(TILES):
                    mm = pe.matmul(pair[2][0:ROWS, t * l.E:(t + 1) * l.E], x2T[:, t, :], selT[l.name][:, :],
                                   start=True, stop=True)
                mm.then_inc(s.lg_ps, 1)

            def r3(l, g, h, j):
                s = S[l.name]
                pe.wait_ge(s.oh_ready, g + 1)
                out_ = pair[2][0:ROWS, 0:TILES * l.E].rearrange("p (t e) -> p t e", t=TILES)
                pe.matmul(out_, before16[0:ROWS, 0:ROWS], ohs[:, :, 0:l.E], start=True, stop=False,
                          skip_group_check=True)
                for t in range(TILES - 1):
                    pe.matmul(out_[:, t + 1:, :], ones16[0:ROWS, 0:ROWS],
                              ohs[:, t:t + 1, 0:l.E].to_broadcast([ROWS, TILES - 1 - t, l.E]),
                              start=False, stop=False, skip_group_check=True)
                pe.matmul(out_, ones16[0:ROWS, 0:ROWS],
                          seen[:, None, 0:l.E].to_broadcast([ROWS, TILES, l.E]),
                          start=False, stop=True, skip_group_check=True).then_inc(s.rank_ps, 1)

            def tables(l):
                s = S[l.name]
                pe.wait_ge(s.slot_ready, GROUPS)
                pe.matmul(pair[0][0:l.E, 0:1], seen[:, 0:l.E], ones16[0:ROWS, 0:1], start=True, stop=True)
                pe.matmul(pair[1][0:1, 0:l.E], ones16[0:ROWS, 0:1], seen[:, 0:l.E], start=True, stop=True)\
                    .then_inc(T.cnt_ps, 1)
                pe.wait_ge(T.nb_ready, l.turn)
                pe.matmul(pair[2][0:l.E, 0:1], upto[0:l.E, 0:l.E], tb.nb[0:l.E, :], start=True, stop=True)\
                    .then_inc(T.cb_ps, 1)
                pe.wait_ge(T.ge_ready, l.turn)
                pe.matmul(pair[0][0:1, 0:l.blocks], tb.v[0:l.E, 0:1], tb.ge[0:l.E, 0:l.blocks], start=True, stop=True)
                pe.matmul(pair[1][0:1, 0:l.blocks], tb.v[0:l.E, 1:2], tb.ge[0:l.E, 0:l.blocks], start=True, stop=True)\
                    .then_inc(T.tab_ps, 1)

            def expert_blocks(l):
                k = K[l.name]
                U = l.unroll
                n_tok = l.block

                def bank_x(i2):
                    return ps[:, i2, 0:n_tok]

                def bank_h(i2, f):
                    b = 2 + 2 * i2 + f // 2
                    return ps[:, b, f % 2 * n_tok:f % 2 * n_tok + n_tok]

                def turn(u, n, j):
                    return (u + n) % U, j + (u + n) // U

                def t1(u, j, n):
                    b, jj = turn(u, n, j)
                    pe.wait_ge(k.blk_in[b], 32 * (k.j0 + jj + 1))
                    for q in range(l.Q):
                        mm = pe.transpose(ps[:, (u + n) % 2, q * 128:(q + 1) * 128], xblk[b][:, q, 0:D], ident[:, :])
                    mm.then_inc(k.xT_ps, 1)

                def t2(u, j, n):
                    b, jj = turn(u, n, j)
                    i = U * j + u + n
                    p2 = i_par(u, n)
                    pe.wait_ge(k.xT_ready, k.i0 + i + 1)
                    for f in range(l.FC):
                        cols_f = slice(f * 128, (f + 1) * 128)
                        if l is L0:
                            mm = pe.matmul(bank_h(p2, f), wblk[b][:, cols_f], xTb[p2][:, 0:n_tok], start=True,
                                           stop=True)
                        else:
                            for n2, (w, x) in enumerate(((w1lo, xbhi), (w1hi, xblo), (w1hi, xbhi))):
                                mm = pe.matmul(bank_h(p2, f), w[p2][:, cols_f], x[p2], start=(n2 == 0),
                                               stop=(n2 == 2), skip_group_check=True)
                    mm.then_inc(k.h_ps, 1)

                def t3(u, j, n):
                    b, jj = turn(u, n, j)
                    i = U * j + u + n
                    p2 = i_par(u, n)
                    pe.wait_ge(k.h_ready, k.i0 + i + 1)
                    if not (isinstance(i, int) and i < 2):
                        pe.wait_ge(k.y_ready, k.i0 + i - 1)
                    w2 = wblk[b][:, l.FC * 128:2 * l.FC * 128]
                    for q in range(l.Q):
                        o = ps[:, 6 + p2, q * D:(q + 1) * D]
                        for f in range(l.FC):
                            mm = pe.matmul(o, hTb[p2][:, f, q * 128:(q + 1) * 128], w2[:, f * D:(f + 1) * D],
                                           start=(f == 0), stop=(f == l.FC - 1))
                    mm.then_inc(k.y_ps, 1)

                def i_par(u, n):
                    return (u + n) % 2

                rounds = l.blocks // U
                t1(0, 0, 0)
                t1(0, 0, 1)
                t2(0, 0, 0)

                def step(u, j, last):
                    if not (last and u + 2 >= U):
                        t1(u, j, 2)
                    if not (last and u + 1 >= U):
                        t2(u, j, 1)
                    t3(u, j, 0)
                for u in range(U):
                    step(u, 0, False)
                with pe.Fori(1, rounds - 1) as j:
                    for u in range(U):
                        step(u, j, False)
                for u in range(U):
                    step(u, rounds - 1, True)

            def step(g, h, j, ahead_a, ahead_e):
                o, jo = 1 - h, j + h

                def tiles(first, end):
                    if ahead_e:
                        embed(g + 2, h, j + 1, first, end)
                tiles(0, 3)
                b1(g, h, j)
                if ahead_a:
                    a1(g + 1, o, jo)
                tiles(3, 4)
                b2(g, h, j)
                tiles(4, 9)
                if ahead_a:
                    a2(g + 1, o, jo)
                tiles(9, 11)
                if ahead_a:
                    a3(g + 1, o, jo)
                r1(L0, g, h, j)
                tiles(11, 11)
                if ahead_a:
                    a4(g + 1, o, jo)
                r2(L0, g, h, j)
                tiles(11, KT)
                r3(L0, g, h, j)

            embed(0, 0, 0, 0, KT - 1)
            pe.wait_ge(w_rest_in, 16)
            embed(0, 0, 0, KT - 1, KT)
            pe.wait_ge(consts_in, 16 * NCONST)
            pe.wait_ge(made, 1)
            pe.wait_ge(consts_dve, 1)
            for f, first in ((a1, 0), (a2, 6), (a3, 10), (a4, 13)):
                f(0, 0, 0)
                embed(1, 1, 0, first, {0: 6, 6: 10, 10: 13, 13: KT}[first])
            for h in range(2):
                step(h, h, 0, True, True)
            with pe.Fori(1, GROUPS // 2 - 1) as j:
                for h in range(2):
                    step(2 * j + h, h, j, True, True)
            j = GROUPS // 2 - 1
            step(2 * j, 0, j, True, False)
            step(2 * j + 1, 1, j, False, False)
            tables(L0)
            expert_blocks(L0)

            def c1(g, h, j):
                pe.wait_ge(m_ntok, g + 1)
                pe.wait_ge(actx_ready, g)
                T_from_tok(lambda t: ntok[:, t, :], 0).then_inc(m_xT_ps, 1)

            def c2(g, h, j):
                pe.wait_ge(ctx_ready, g + 1)
                tok_from_T(ctxT[:, :, :].rearrange("p i t -> p (i t)"), 0).then_inc(ctx_ps, 1)

            def c3(g, h, j):
                pe.wait_ge(delta_ready, g + 1)
                pe.wait_ge(ssq_ready, g)
                tok_from_T(cumT[:, :, :].rearrange("p i t -> p (i t)"), 1).then_inc(delta_ps, 1)

            def mid_step(g, h, j, ahead):
                o, jo = 1 - h, j + h
                if ahead:
                    c1(g + 1, o, jo)
                r1(L1, g, h, j)
                if ahead:
                    c2(g + 1, o, jo)
                r2(L1, g, h, j)
                if ahead:
                    c3(g + 1, o, jo)
                r3(L1, g, h, j)

            for f in (c1, c2, c3):
                f(0, 0, 0)
            for h in range(2):
                mid_step(h, h, 0, True)
            with pe.Fori(1, GROUPS // 2 - 1) as j:
                for h in range(2):
                    mid_step(2 * j + h, h, j, True)
            j = GROUPS // 2 - 1
            mid_step(2 * j, 0, j, True)
            mid_step(2 * j + 1, 1, j, False)
            tables(L1)
            expert_blocks(L1)

        @block.scalar
        def _(act):
            act.dma_start(w_emb[:, :, :].rearrange("p k d -> p (k d)"), a["w_main"]).then_inc(w_emb_in, 16)
            act.dma_start(w_rest[:, :], a["w_rest"]).then_inc(w_rest_in, 16)
            act.dma_start(small[:, :], a["small"]).then_inc(consts_in, 16)
            act.dma_start(per_row[:, :], a["per_row"].to_broadcast([128, D + L1.E + 1])).then_inc(consts_in, 16)
            def high(g, h, j):
                act.wait_ge(chunk_in[h][SPLIT], 32 * (j + 1))
                if not (isinstance(g, int) and g == 0):
                    act.wait_ge(chunk_used[1 - h][SPLIT], j + h)
                act.activation(x_hi[:, :, :].rearrange("p k n -> p (k n)"),
                               xin[h][SPLIT][:, :, :].rearrange("p k n -> p (k n)"), ACT.Copy).then_inc(x_hi_ready, 1)

            act.wait_ge(w_emb_in, 16)
            act.activation(w_hi[:, :, :].rearrange("p k d -> p (k d)"),
                           w_emb[:, SPLIT * KC:KT, :].rearrange("p k d -> p (k d)"), ACT.Copy).then_inc(w_hi_ready, 1)
            high(0, 0, 0)
            act.wait_ge(consts_in, 16 * NCONST)
            act.activation(kcol[:, 1:2], per_row[:, D + L1.E:], ACT.Exp).then_inc(exp_ready, 1)

            def copy(dst, src):
                return act.activation(dst, src, ACT.Copy)

            def flat(tile):
                return tile.rearrange("p t d -> p (t d)")

            def a1(g, h, j):
                act.wait_ge(h0_ps, g + 1)
                act.wait_ge(ntok_ready, g)
                copy(flat(atok[:, :, :]), pair[0][0:ROWS, 0:TILES * D]).then_inc(atok_ready, 1)

            def a2(g, h, j):
                act.wait_ge(xT_ps, g + 1)
                copy(x1T[h][:, :].rearrange("p (t r) -> p t r", t=TILES),
                     pair[0][:, 0:TILES * 128].rearrange("p (t r) -> p t r", t=TILES)[:, :, 0:ROWS])\
                    .then_inc(x1T_ready, 1)

            def a3(g, h, j):
                act.wait_ge(q_ps, g + 1)
                act.activation(QT[:, :].rearrange("p (n r) -> p n r", n=2),
                               pair[0].rearrange("p (n r) -> p n r", n=2)[:, :, 0:HALF],
                               ACT.Identity, bias=cols[:, 1:2]).then_inc(q_ready, 1)
                act.wait_ge(k_ps, g + 1)
                act.wait_ge(s_ps, g)
                act.activation(KTt[:, :].rearrange("p (n r) -> p n r", n=2),
                               pair[1].rearrange("p (n r) -> p n r", n=2)[:, :, 0:HALF],
                               ACT.Identity, bias=cols[:, 2:3]).then_inc(k_ready, 1)

            def a4(g, h, j):
                act.wait_ge(shifted, g + 1)
                act.activation(Pr[h][:, :, :].rearrange("p i t -> p (i t)"), Sm[:, :, :].rearrange("p i t -> p (i t)"),
                               ACT.Exp).then_inc(exp_ready, 1)

            def b2(g, h, j):
                s = S["L0"]
                act.wait_ge(hT_ps, g + 1)
                act.wait_ge(s.resid_out[h], 16 * j)
                copy(flat(htok[h][:, :, :]), pair[2][0:ROWS, 0:TILES * D]).then_inc(s.htok_ready, 1)
                act.wait_ge(s.htok_ready, g + 1)
                act.dma_start(resid["L0"][bass.ds(g, 1), :, :].rearrange("o p n -> (o p) n"),
                              flat(htok[h][:, :, :])).then_inc(s.resid_out[h], 16)

            def r1(l, g, h, j):
                s = S[l.name]
                act.wait_ge(s.x2T_ps, g + 1)
                copy(x2T[:, :, :], pair[2][:, 0:TILES * 128].rearrange("p (t r) -> p t r", t=TILES)[:, :, 0:ROWS])\
                    .then_inc(s.x2T_ready, 1)
                act.wait_ge(s.rows0_ready, g + 1)
                copy(rows[h][:, :, 1, 0:D], rows[h][:, :, 0, 0:D]).then_inc(s.rows1_ready, 1)

            def r2(l, g, h, j):
                s = S[l.name]
                act.wait_ge(s.top_ready, g + 1)
                if l is L0:
                    act.activation(eg[:, :, :], top8[:, :, 0:TOP], ACT.Exp, scale=-1.0).then_inc(s.eg_ready, 1)
                else:
                    act.activation(lgs[:, :, 0:l.E], lgs[:, :, 0:l.E], ACT.Exp)
                    act.activation(eg[:, :, :], eg[:, :, :], ACT.Exp).then_inc(s.eg_ready, 1)

            def front_step(g, h, j, ahead, ahead_e=True):
                o, jo = 1 - h, j + h
                if ahead:
                    a1(g + 1, o, jo)
                b2(g, h, j)
                if ahead_e:
                    high(g + 2, h, j + 1)
                if ahead:
                    a2(g + 1, o, jo)
                    a3(g + 1, o, jo)
                r1(L0, g, h, j)
                if ahead:
                    a4(g + 1, o, jo)
                r2(L0, g, h, j)

            a1(0, 0, 0)
            high(1, 1, 0)
            for f in (a2, a3, a4):
                f(0, 0, 0)
            for h in range(2):
                front_step(h, h, 0, True)
            with act.Fori(1, GROUPS // 2 - 1) as j:
                for h in range(2):
                    front_step(2 * j + h, h, j, True)
            j = GROUPS // 2 - 1
            front_step(2 * j, 0, j, True, False)
            front_step(2 * j + 1, 1, j, False, False)

            def expert_blocks(l):
                k = K[l.name]
                U = l.unroll

                def xT(u, j, n):
                    i = U * j + u + n
                    p2 = (u + n) % 2
                    act.wait_ge(k.xT_ps, k.i0 + i + 1)
                    if not (isinstance(i, int) and i < 2):
                        act.wait_ge(k.h_ps, k.i0 + i - 1)
                    copy(xTb[p2][:, 0:l.block], ps[:, p2, 0:l.block]).then_inc(k.xT_ready, 1)

                def gelu(u, j, n):
                    i = U * j + u + n
                    p2 = (u + n) % 2
                    b = (u + n) % U
                    act.wait_ge(k.h_ps, k.i0 + i + 1)
                    if not (isinstance(i, int) and i < 2):
                        act.wait_ge(k.y_ps, k.i0 + i - 1)
                    for f in range(l.FC):
                        b1 = wblk[b][:, 2 * l.FC * 128 + f:2 * l.FC * 128 + f + 1]
                        ins = act.activation(hTb[p2][:, f, 0:l.block],
                                             ps[:, 2 + 2 * p2 + f // 2, f % 2 * l.block:(f % 2 + 1) * l.block],
                                             ACT.Gelu, bias=b1)
                    ins.then_inc(k.h_ready, 1)

                def high(u, j, n):
                    i = U * j + u + n
                    act.wait_ge(k.blk_in[(u + n) % U], 32 * (k.j0 + j + (u + n) // U + 1))
                    if not (isinstance(i, int) and i < 2):
                        act.wait_ge(k.h_ps, k.i0 + i - 1)
                    copy(w1hi[(u + n) % 2], wblk[(u + n) % U][:, 0:l.FC * 128])\
                        .then_inc(w1hi_ready, 1)

                works = [(xT, 2)] if l is L0 else [(high, 2), (gelu, 1)]
                for f, lead in works:
                    for n in range(lead):
                        f(0, 0, n)
                for u in range(U):
                    for f, lead in works:
                        f(u, 0, lead)
                with act.Fori(1, l.blocks // U - 1) as j:
                    for u in range(U):
                        for f, lead in works:
                            f(u, j, lead)
                for u in range(U):
                    for f, lead in works:
                        if u < U - lead:
                            f(u, l.blocks // U - 1, lead)

            pads(act, L0, 1)
            expert_blocks(L0)

            def c1(g, h, j):
                act.wait_ge(m_xT_ps, g + 1)
                act.wait_ge(delta_ready, g)
                act.wait_ge(ctx_ready, g)
                copy(xc[:, :, :].rearrange("p i t -> p (i t)").rearrange("p (t r) -> p t r", t=TILES),
                     pair[0][:, 0:TILES * 128].rearrange("p (t r) -> p t r", t=TILES)[:, :, 0:ROWS])\
                    .then_inc(m_xc, 1)

            def c2(g, h, j):
                act.wait_ge(delta_ps, g + 1)
                act.wait_ge(mag_ready, g)
                for t in range(TILES):
                    ins = act.activation(sq[:, t, :], pair[1][0:ROWS, t * D:(t + 1) * D], ACT.Square,
                                         accum_out=ssq[:, t:t + 1])
                ins.then_inc(ssq_ready, 1)
                act.wait_ge(mag_ready, g + 1)
                act.wait_ge(ctx_ps, g + 1)
                act.wait_ge(S["L1"].htok_ready, g)
                for t in range(TILES):
                    ins = act.activation(actx[:, t, :], pair[0][0:ROWS, t * D:(t + 1) * D], ACT.Abs,
                                         scale=mag[:, t:t + 1])
                ins.then_inc(actx_ready, 1)

            def c3(g, h, j):
                s = S["L1"]
                act.wait_ge(s.htok_ready, g + 1)
                act.dma_start(resid["L1"][bass.ds(g, 1), :, :].rearrange("o p n -> (o p) n"),
                              flat(htok[h][:, :, :])).then_inc(s.resid_out[h], 16)

            def mid_step(g, h, j, ahead):
                o, jo = 1 - h, j + h
                if ahead:
                    c1(g + 1, o, jo)
                r1(L1, g, h, j)
                r2(L1, g, h, j)
                if ahead:
                    c2(g + 1, o, jo)
                    c3(g + 1, o, jo)

            for f in (c1, c2, c3):
                f(0, 0, 0)
            for h in range(2):
                mid_step(h, h, 0, True)
            with act.Fori(1, GROUPS // 2 - 1) as j:
                for h in range(2):
                    mid_step(2 * j + h, h, j, True)
            j = GROUPS // 2 - 1
            mid_step(2 * j, 0, j, True)
            mid_step(2 * j + 1, 1, j, False)
            pads(act, L1, 1)
            expert_blocks(L1)
            def store(g, u, j):
                act.wait_ge(e_ready, g + 1)
                act.dma_start(out.rearrange("(g t p) d -> g p t d", g=GROUPS, p=ROWS)[bass.ds(g, 1), :, :, :]
                              .rearrange("o p t d -> (o p) t d"), fin[u][:, :, :]).then_inc(e_out[u], 16)
            ring(act, store)
            for u in range(NE):
                act.wait_ge(e_out[u], 16 * GROUPS // NE)

        @block.vector
        def _(dve):
            def low(g, h, j):
                dve.wait_ge(x_hi_ready, g + 1)
                x = xin[h][SPLIT][:, :, :].rearrange("p k n -> p (k n)")
                dve.tensor_tensor(x_lo[:, :, :].rearrange("p k n -> p (k n)"), x,
                                  x_hi[:, :, :].rearrange("p k n -> p (k n)").bitcast(F32), ALU.subtract)\
                    .then_inc(split, 1)

            dve.wait_ge(w_hi_ready, 1)
            w = w_emb[:, SPLIT * KC:KT, :].rearrange("p k d -> p (k d)")
            dve.tensor_tensor(w_lo[:, :, :].rearrange("p k d -> p (k d)"), w,
                              w_hi[:, :, :].rearrange("p k d -> p (k d)").bitcast(F32), ALU.subtract)\
                .then_inc(split, 1)
            low(0, 0, 0)
            dve.wait_ge(consts_in, 16 * NCONST)
            dve.wait_ge(made, 1)
            st = Steps(1)
            for h in range(2):
                ins = dve.tensor_scalar(h0T[h][:, :, 0:1], h0T[h][:, :, 0:1], cols[:, 3:4], posT[:, 0:1],
                                        ALU.add, ALU.mult)
            ins.then_inc(consts_dve, 1)

            def norm_stats(ln, x, st, step, stats):
                for t in range(TILES):
                    ins = dve.bn_stats(ln.bn[:, t, :], x[:, t, :])
                ins.then_inc(step, st.one())
                dve.wait_ge(step, st.all())
                past(dve, dve_passed)
                for t in range(TILES):
                    ins = dve.bn_aggr(ln.mv[:, t, :], ln.bn[:, t, :])
                ins.then_inc(stats, 1)

            def norm_apply(ln, x, y):
                for t in range(TILES):
                    ins = dve.tensor_scalar(y(t), x[:, t, :], ln.mv[:, t, 0:1], ln.rs[:, t:t + 1],
                                            ALU.subtract, ALU.mult)
                return ins

            NA, NBB, NR = 5, 1, {"L0": 9, "L1": 12}

            def e0(g, h, j):
                dve.wait_ge(chunk_used[h][CHUNKS - 1], j + 1)
                dve.scalar_tensor_tensor(h0T[h][:, :, 1:], psE[h].rearrange("p (i n) -> p i n", i=GI), cols[:, 0:1],
                                         posT[:, None, 1:].to_broadcast([D, GI, PATCHES]), ALU.add, ALU.mult)\
                    .then_inc(h0T_ready, 1)

            def a1(g, h, j):
                st = Steps(NA * g)
                dve.wait_ge(atok_ready, g + 1)
                norm_stats(LNA, atok, st, dveA, statsA)

            def a1_apply(g, h, j):
                dve.wait_ge(rstdA, g + 1)
                dve.wait_ge(statsA, g + 1)
                dve.wait_ge(xT_ps, g)
                norm_apply(LNA, atok, lambda t: ntok[:, t, :]).then_inc(ntok_ready, 1)

            def a2(g, h, j):
                dve.wait_ge(v_ps, g + 1)
                dve.tensor_tensor(V[h][:, :, :], pair[0][0:SEQ, :].rearrange("p (i d) -> p i d", i=GI),
                                  bv_rows[:, None, :].to_broadcast([SEQ, GI, D]), ALU.add).then_inc(v_ready, 1)

            def a3(g, h, j):
                st = Steps(NA * g + 1)
                dve.wait_ge(s_ps, g + 1)
                dve.wait_ge(exp_ready, g + 1)
                S4 = Sm[:, :, :].rearrange("p (n i) t -> p n i t", n=2)
                pv = pair[1][0:SEQ, :].rearrange("p (n r) -> p n r", n=2)[:, :, 0:HALF]\
                    .rearrange("p n (i t) -> p n i t", i=4)
                for n in range(2):
                    ins = dve.tensor_tensor(S4[:, n], pv[:, n], causal[:, None, :].to_broadcast([SEQ, 4, SEQ]),
                                            ALU.add)
                ins.then_inc(s_read, 1)
                dve.wait_ge(s_read, g + 1)
                dve.tensor_reduce(smax[:, :], Sm[:, :, :], X, ALU.max).then_inc(dveA, st.one())
                dve.wait_ge(dveA, st.all())
                dve.tensor_tensor(Sm[:, :, :], Sm[:, :, :], smax[:, :, None].to_broadcast([SEQ, GI, SEQ]),
                                  ALU.subtract).then_inc(shifted, 1)

            def a4(g, h, j):
                st = Steps(NA * g + 2)
                dve.wait_ge(exp_ready, g + 2)
                dve.tensor_reduce(ssum[:, :], Pr[h][:, :, :], X, ALU.add).then_inc(dveA, st.one())
                dve.wait_ge(dveA, st.all())
                dve.reciprocal(ssum[:, :], ssum[:, :]).then_inc(dveA, st.one())
                dve.wait_ge(dveA, st.all())
                dve.tensor_scalar(ssum[:, :], ssum[:, :], float(D) ** -0.5, None, ALU.mult).then_inc(dveA, st.one())
                dve.wait_ge(dveA, st.all())
                dve.tensor_tensor(Pr[h][:, :, :], Pr[h][:, :, :], ssum[:, :, None].to_broadcast([SEQ, GI, SEQ]),
                                  ALU.mult).then_inc(p_ready, 1)

            def b1(g, h, j):
                st = Steps(NBB * g)
                dve.wait_ge(read_ps, g + 1)
                dve.wait_ge(x1T_ready, g + 1)
                dve.wait_ge(hT_ps, g)
                dve.tensor_tensor(u0T[:, :], h0T[h][:, :, :].rearrange("p i t -> p (i t)"), x1T[h][:, :],
                                            ALU.add).then_inc(dveB, st.one())
                dve.wait_ge(dveB, st.all())
                dve.tensor_tensor(h1T[:, :].rearrange("p (n r) -> p n r", n=2),
                                  u0T[:, :].rearrange("p (n r) -> p n r", n=2),
                                  pair[2].rearrange("p (n r) -> p n r", n=2)[:, :, 0:HALF], ALU.add)\
                    .then_inc(h1T_ready, 1)

            def r1(l, g, h, j):
                s = S[l.name]
                st = Steps(NR[l.name] * g)
                dve.wait_ge(s.htok_ready, g + 1)
                norm_stats(LNB, htok[h], st, s.dveR, s.statsB)

            def r1_apply(l, g, h, j):
                s = S[l.name]
                dve.wait_ge(s.rstdB, g + 1)
                dve.wait_ge(s.statsB, g + 1)
                dve.wait_ge(s.scattered[h], 16 * TILES * TOP * j)
                norm_apply(LNB, htok[h], lambda t: rows[h][:, t, 0, 0:D]).then_inc(s.rows0_ready, 1)

            def r2(l, g, h, j):
                s = S[l.name]
                st = Steps(NR[l.name] * g + 1)
                E = l.E
                dve.wait_ge(s.lg_ps, g + 1)
                logit = pair[2][0:ROWS, 0:TILES * E].rearrange("p (t e) -> p t e", t=TILES)
                if l is L0:
                    dve.tensor_copy(lg[:, :, 0:E], logit).then_inc(s.dveR, st.one())
                else:
                    dve.tensor_tensor(lg[:, :, 0:E], logit,
                                                rb_rows[:, None, :].to_broadcast([ROWS, TILES, E]), ALU.add).then_inc(s.dveR, st.one())
                dve.wait_ge(s.dveR, st.all())
                dve.wait_ge(s.eg_ready, g)
                past(dve, dve_passed)
                for t in range(TILES):
                    ins = dve.max(top8[:, t, :], lg[:, t, 0:E])
                if l is L0:
                    ins.then_inc(s.top_ready, 1)
                    dve.wait_ge(s.top_ready, g + 1)
                else:
                    ins.then_inc(s.dveR, st.one())
                    dve.wait_ge(s.dveR, st.all())
                if l is L1:
                    dve.tensor_tensor(lgs[:, :, 0:E], lg[:, :, 0:E],
                                                top8[:, :, 0:1].to_broadcast([ROWS, TILES, E]), ALU.subtract).then_inc(s.dveR, st.one())
                    dve.tensor_tensor(eg[:, :, :], top8[:, :, 0:TOP], top8[:, :, 0:1].to_broadcast([ROWS, TILES, TOP]),
                                      ALU.subtract).then_inc(s.top_ready, 1)
                past(dve, dve_passed)
                for t in range(TILES):
                    ins = dve.max_index(idx8[:, t, :], top8[:, t, :], lg[:, t, 0:E])
                ins.then_inc(s.dveR, st.one())
                dve.wait_ge(s.dveR, st.all())
                dve.tensor_copy(chosen[:, :, :], idx8[:, :, 0:TOP]).then_inc(s.dveR, st.one())
                dve.wait_ge(s.dveR, st.all())
                for k in range(TOP):
                    ins = dve.tensor_tensor(oh[:, :, k, 0:E], iotaE[:, None, 0:E].to_broadcast([ROWS, TILES, E]),
                                            chosen[:, :, k:k + 1].to_broadcast([ROWS, TILES, E]), ALU.is_equal)
                ins.then_inc(s.dveR, st.one())
                dve.wait_ge(s.dveR, st.all())
                dve.wait_ge(s.rank_ps, g)
                dve.tensor_tensor(ohs[:, :, 0:E], oh[:, :, 0, 0:E], oh[:, :, 1, 0:E], ALU.add).then_inc(s.oh_ready, 1)
                dve.wait_ge(s.eg_ready, g + 1)
                if l is L0:
                    dve.tensor_scalar(eg[:, :, :], eg[:, :, :], 1.0, None, ALU.add).then_inc(s.dveR, st.one())
                    dve.wait_ge(s.dveR, st.all())
                    dve.reciprocal(rows[h][:, :, :, GATE], eg[:, :, :]).then_inc(s.gate_ready, 1)
                else:
                    dve.tensor_reduce(gsum[:, :], lgs[:, :, 0:E], X, ALU.add).then_inc(s.dveR, st.one())
                    dve.wait_ge(s.dveR, st.all())
                    dve.reciprocal(gsum[:, :], gsum[:, :]).then_inc(s.dveR, st.one())
                    dve.wait_ge(s.dveR, st.all())
                    dve.tensor_tensor(rows[h][:, :, :, GATE], eg[:, :, :],
                                      gsum[:, :, None].to_broadcast([ROWS, TILES, TOP]), ALU.mult)\
                        .then_inc(s.gate_ready, 1)
                return st

            def r3(l, g, h, j, st):
                s = S[l.name]
                E = l.E
                dve.wait_ge(s.oh_ready, g + 1)
                dve.tensor_reduce(added[:, 0:E], ohs[:, :, 0:E].rearrange("p t e -> p e t"), X, ALU.add).then_inc(s.dveR, st.one())
                dve.wait_ge(s.rank_ps, g + 1)
                rk = pair[2][0:ROWS, 0:TILES * E].rearrange("p (t e) -> p t e", t=TILES)
                for k in range(TOP):
                    ins = dve.tensor_tensor(pick[:, :, k, 0:E], rk, oh[:, :, k, 0:E], ALU.mult)
                ins.then_inc(s.rank_read, 1)

            def r3_slots(l, g, h, j, st):
                s = S[l.name]
                E = l.E
                dve.wait_ge(s.rank_read, g + 1)
                dve.wait_ge(s.dveR, st.all())
                dve.tensor_tensor(seen[:, 0:E], seen[:, 0:E], added[:, 0:E], ALU.add).then_inc(s.dveR, st.one())
                dve.wait_ge(s.dveR, st.all())
                dve.tensor_reduce(rank[:, :, :], pick[:, :, :, 0:E], X, ALU.add).then_inc(s.dveR, st.one())
                dve.wait_ge(s.dveR, st.all())
                dve.scalar_tensor_tensor(slots[h][:, :, :], chosen[:, :, :], float(l.room), rank[:, :, :],
                                         ALU.mult, ALU.add).then_inc(s.slot_ready, 1)
                dve.wait_ge(s.slot_ready, g + 1)

            def front_step(g, h, j, ahead_a, ahead_e):
                o, jo = 1 - h, j + h
                b1(g, h, j)
                if ahead_a:
                    a1(g + 1, o, jo)
                r1(L0, g, h, j)
                if ahead_a:
                    a1_apply(g + 1, o, jo)
                r1_apply(L0, g, h, j)
                if ahead_e:
                    low(g + 2, h, j + 1)
                if ahead_a:
                    a2(g + 1, o, jo)
                    a3(g + 1, o, jo)
                st = r2(L0, g, h, j)
                if ahead_a:
                    a4(g + 1, o, jo)
                r3(L0, g, h, j, st)
                if ahead_e:
                    e0(g + 2, h, j + 1)
                r3_slots(L0, g, h, j, st)
                assert st.n + 1 == NR["L0"], st.n

            dve.wait_ge(made, 1)
            dve.wait_ge(consts_dve, 1)
            e0(0, 0, 0)
            a1(0, 0, 0)
            a1_apply(0, 0, 0)
            low(1, 1, 0)
            for f in (a2, a3, a4):
                f(0, 0, 0)
            e0(1, 1, 0)
            for h in range(2):
                front_step(h, h, 0, True, True)
            with dve.Fori(1, GROUPS // 2 - 1) as j:
                for h in range(2):
                    front_step(2 * j + h, h, j, True, True)
            j = GROUPS // 2 - 1
            front_step(2 * j, 0, j, True, False)
            front_step(2 * j + 1, 1, j, False, False)

            def tables(l):
                s = S[l.name]
                E, n = l.E, l.blocks
                st = Steps(9 * (l.turn - 1))

                def link(ins):
                    ins.then_inc(T.table_step, st.one())
                    dve.wait_ge(T.table_step, st.all())
                dve.wait_ge(T.cnt_ps, l.turn)
                dve.scalar_tensor_tensor(tb.fr[:, 0:E], iotaB[0:1, 0:E], float(l.room), pair[1][0:1, 0:E],
                                         ALU.mult, ALU.add).then_inc(T.fr_ready, 1)
                link(dve.tensor_copy(tb.cnt[0:E, :], pair[0][0:E, 0:1]))
                link(dve.tensor_scalar(tb.up[0:E, :], tb.cnt[0:E, :], float(l.block - 1), None, ALU.add))
                link(dve.tensor_scalar(tb.up[0:E, :], tb.up[0:E, :], l.shift, None, ALU.arith_shift_right))
                dve.tensor_copy(tb.nb[0:E, :], tb.up[0:E, :]).then_inc(T.nb_ready, 1)
                dve.wait_ge(T.nb_ready, l.turn)
                link(dve.tensor_scalar(tb.v[0:E, 1:2], tb.nb[0:E, :], float(-l.block), float(l.room), ALU.mult, ALU.add))
                link(dve.memset(tb.v[0:E, 0:1], 1.0))
                dve.wait_ge(T.cb_ps, l.turn)
                link(dve.tensor_copy(tb.cb[0:E, :], pair[2][0:E, 0:1]))
                dve.tensor_scalar(tb.ge[0:E, 0:n], iotaB[0:E, 0:n], tb.cb[0:E, :], None, ALU.is_ge)\
                    .then_inc(T.ge_ready, 1)
                dve.wait_ge(T.tab_ps, l.turn)
                link(dve.tensor_scalar(tb.ef[:, 0:n], pair[0][0:1, 0:n], float(E - 1), None, ALU.min))
                link(dve.scalar_tensor_tensor(tb.rf[:, 0:n], iotaB[0:1, 0:n], float(l.block), pair[1][0:1, 0:n],
                                              ALU.mult, ALU.add))
                link(dve.tensor_scalar(tb.rf[:, 0:n], tb.rf[:, 0:n], float(E * l.room), None, ALU.min))
                dve.scalar_tensor_tensor(tb.entry[:, 0:n], tb.ef[:, 0:n], float(l.step), tb.rf[:, 0:n],
                                         ALU.mult, ALU.add).then_inc(T.tables_ready, 1)
                assert st.n == 9, st.n

            tables(L0)

            def expert_blocks(l):
                k = K[l.name]
                U = l.unroll

                def relu(u, j, n):
                    i = U * j + u + n
                    p2 = (u + n) % 2
                    dve.wait_ge(k.h_ps, k.i0 + i + 1)
                    if not (isinstance(i, int) and i < 2):
                        dve.wait_ge(k.y_ps, k.i0 + i - 1)
                    dve.tensor_scalar(hTb[p2][:, 0, 0:l.block], ps[:, 2 + 2 * p2, 0:l.block], 0.0, None, ALU.max)\
                        .then_inc(k.h_ready, 1)

                def xT(u, j, n):
                    i = U * j + u + n
                    p2 = (u + n) % 2
                    dve.wait_ge(k.xT_ps, k.i0 + i + 1)
                    if not (isinstance(i, int) and i < 2):
                        dve.wait_ge(k.h_ps, k.i0 + i - 1)
                    dve.tensor_copy(xbhi[p2], ps[:, p2, 0:l.block]).then_inc(xhi_ready, 1)
                    w1 = wblk[(u + n) % U][:, 0:l.FC * 128]
                    dve.wait_ge(w1hi_ready, i + 1)
                    dve.tensor_tensor(w1lo[p2], w1, w1hi[p2].bitcast(F32), ALU.subtract)
                    dve.wait_ge(xhi_ready, i + 1)
                    dve.tensor_tensor(xblo[p2], ps[:, p2, 0:l.block], xbhi[p2].bitcast(F32), ALU.subtract)\
                        .then_inc(k.xT_ready, 1)

                def gated(u, j):
                    i = U * j + u
                    p2 = u % 2
                    dve.wait_ge(k.y_ps, k.i0 + i + 1)
                    dve.wait_ge(k.y_out[u], k.y0 + 16 * l.Q * j)
                    y = ps[:, 6 + p2, 0:l.Q * D].rearrange("p (q d) -> p q d", q=l.Q)
                    gate = xblk[u][:, 0:l.Q, GATE:GATE + 1].to_broadcast([128, l.Q, D])
                    if l.FC > 1:
                        dve.tensor_tensor(yblk[u][:, :, :], y,
                                          wblk[u][:, None, l.W - D:l.W].to_broadcast([128, l.Q, D]), ALU.add)\
                            .then_inc(y_biased, 1)
                        dve.wait_ge(y_biased, i + 1)
                        y = yblk[u][:, :, :]
                    dve.tensor_tensor(yblk[u][:, :, :], y, gate, ALU.mult).then_inc(k.y_ready, 1)

                f, lead = (relu, 1) if l is L0 else (xT, 2)

                def step(u, j, last):
                    if not (last and u + lead >= U):
                        f(u, j, lead)
                    gated(u, j)
                for n in range(lead):
                    f(0, 0, n)
                for u in range(U):
                    step(u, 0, False)
                with dve.Fori(1, l.blocks // U - 1) as j:
                    for u in range(U):
                        step(u, j, False)
                for u in range(U):
                    step(u, l.blocks // U - 1, True)

            expert_blocks(L0)

            def c0(g, h, j):
                st = Steps(2 * g)
                dve.wait_ge(m_in[h], 32 * (j + 1))
                dve.tensor_tensor(h2tok[h][:, :, :], yin[h][:, :, 0, :], yin[h][:, :, 1, :], ALU.add).then_inc(dveM, st.one())
                dve.wait_ge(dveM, st.all())
                dve.tensor_tensor(h2tok[h][:, :, :], h2tok[h][:, :, :], hin[h][:, :, :], ALU.add)\
                    .then_inc(m_free[h], 1)
                dve.wait_ge(m_free[h], j + 1)
                norm_stats(LNA, h2tok[h], st, dveM, m_statsA)

            def c0_apply(g, h, j):
                dve.wait_ge(m_rstdA, g + 1)
                dve.wait_ge(m_statsA, g + 1)
                dve.wait_ge(m_xT_ps, g)
                norm_apply(LNA, h2tok[h], lambda t: ntok[:, t, :]).then_inc(m_ntok, 1)

            def c1(g, h, j):
                dve.wait_ge(m_xc, g + 1)
                dve.wait_ge(delta_ps, g)
                dve.wait_ge(ctx_ps, g)

                def fl(x):
                    return x[:, :, :].rearrange("p i t -> p (i t)")
                dve.tensor_tensor_scan(fl(cumT), fl(first0), fl(xc), 0.0, ALU.mult, ALU.add).then_inc(scan_step, 1)
                dve.tensor_tensor_scan(fl(ctxT), fl(decay), fl(xc), 0.0, ALU.mult, ALU.add).then_inc(ctx_ready, 1)

            def c1_diff(g, h, j):
                dve.wait_ge(scan_step, g + 1)
                dve.tensor_tensor(cumT[:, :, 1:], cumT[:, :, 1:], xc[:, :, 0:SEQ - 1], ALU.subtract)\
                    .then_inc(delta_ready, 1)

            scan_step = sem("scan_step")

            def c2(g, h, j):
                s = S["L1"]
                dve.wait_ge(actx_ready, g + 1)
                dve.wait_ge(s.resid_out[h], 16 * j)
                dve.tensor_tensor(htok[h][:, :, :], h2tok[h][:, :, :], actx[:, :, :], ALU.add)\
                    .then_inc(s.htok_ready, 1)

            def mid_step(g, h, j, ahead, ahead2=True):
                o, jo = 1 - h, j + h
                if ahead:
                    c0_apply(g + 1, o, jo)
                r1(L1, g, h, j)
                if ahead:
                    c1(g + 1, o, jo)
                r1_apply(L1, g, h, j)
                if ahead:
                    c1_diff(g + 1, o, jo)
                if ahead2:
                    c0(g + 2, h, j + 1)
                st = r2(L1, g, h, j)
                r3(L1, g, h, j, st)
                r3_slots(L1, g, h, j, st)
                if ahead:
                    c2(g + 1, o, jo)
                assert st.n + 1 == NR["L1"], st.n

            ins = dve.memset(seen[:, :], 0.0)
            ins.then_inc(consts_dve, 1)
            dve.wait_ge(exp_ready, GROUPS + 1)
            dve.tensor_scalar(kcol[:, 1:2], kcol[:, 1:2], 1.0, None, ALU.add).then_inc(consts_dve, 1)
            dve.wait_ge(consts_dve, 3)
            dve.reciprocal(kcol[:, 1:2], kcol[:, 1:2]).then_inc(consts_dve, 1)
            dve.wait_ge(consts_dve, 4)
            dve.tensor_scalar(decay[:, :, :], first0[:, :, :], kcol[:, 1:2], None, ALU.mult)\
                .then_inc(consts_dve, 1)
            dve.wait_ge(consts_dve, 5)
            for f in (c0, c0_apply, c1, c1_diff):
                f(0, 0, 0)
            c0(1, 1, 0)
            c2(0, 0, 0)
            for h in range(2):
                mid_step(h, h, 0, True)
            with dve.Fori(1, GROUPS // 2 - 1) as j:
                for h in range(2):
                    mid_step(2 * j + h, h, j, True)
            j = GROUPS // 2 - 1
            mid_step(2 * j, 0, j, True, False)
            mid_step(2 * j + 1, 1, j, False, False)
            tables(L1)
            expert_blocks(L1)
            def total(g, u, j):
                dve.wait_ge(e_in[u], 32 * (j + 1))
                dve.wait_ge(e_out[u], 16 * j)
                dve.tensor_tensor(fin[u][:, :, :], end_y[u][:, :, 0, :], end_y[u][:, :, 1, :], ALU.add)\
                    .then_inc(e_dve, 1)
                dve.wait_ge(e_dve, g + 1)
                dve.tensor_tensor(fin[u][:, :, :], fin[u][:, :, :], end_h[u][:, :, :], ALU.add)\
                    .then_inc(e_ready, 1)
            ring(dve, total)

        @block.gpsimd
        def _(pool):
            n = [0]

            def link(ins):
                n[0] += 1
                ins.then_inc(made_step, 1)
                pool.wait_ge(made_step, n[0])

            def fill(t, value, keep, base, pattern, mult):
                link(pool.affine_select(out=t, in_=t, compare_op=keep, fill=value, base=base, pattern=pattern,
                                        channel_multiplier=mult))
            link(pool.memset(ident[:, :], 0.0))
            fill(ident[:, :], 1.0, ALU.not_equal, 0, [[-1, 128]], 1)
            link(pool.memset(ones[:, :], 1.0))
            link(pool.memset(ones16[:, :], 1.0))
            link(pool.memset(before16[:, :], 1.0))
            fill(before16[:, :], 0.0, ALU.is_gt, 0, [[1, 128]], -1)
            link(pool.memset(upto[:, :], 1.0))
            fill(upto[:, :], 0.0, ALU.is_ge, 0, [[1, 32]], -1)
            link(pool.memset(causal[:, :], 0.0))
            fill(causal[:, :], MASKED, ALU.is_ge, 0, [[1, SEQ]], -1)
            link(pool.iota(iotaE[:, :], pattern=[[1, 32]], base=0, channel_multiplier=0,
                           allow_small_or_imprecise_dtypes=True))
            link(pool.iota(iotaB[:, :], pattern=[[1, 192]], base=0, channel_multiplier=0,
                           allow_small_or_imprecise_dtypes=True))
            link(pool.iota(place0[:, :, :], pattern=[[TOP * ROWS, TILES], [1, TOP]], base=0,
                           channel_multiplier=TOP, allow_small_or_imprecise_dtypes=True))
            link(pool.tensor_copy(place[:, :, :], place0[:, :, :]))
            link(pool.memset(half_m[:, :], -0.5))
            link(pool.memset(half_p[:, :], 0.5))
            link(pool.memset(seen[:, :], 0.0))
            link(pool.memset(padrows[:, :, :], 0.0))
            link(pool.memset(padrows[:, :, PLACE:PLACE + 1].bitcast(I32), NOWHERE))
            for h in range(2):
                link(pool.memset(rows[h][:, :, :, D:ROW], 0.0))
                link(pool.memset(h0T[h][:, :, 0:1], 0.0))
            link(pool.memset(first0[:, :, :], 1.0))
            pool.memset(first0[:, :, 0:1], 0.0).then_inc(made, 1)
            last = pool.to_reg(TOKENS * TOP - 1)

            def rstd(ln, g, stats, ready, steps):
                pool.wait_ge(stats, g + 1)
                past(pool, pool_passed)
                pool.tensor_scalar(ln.ve[:, :], ln.mv[:, :, 1], EPS, None, ALU.add).then_inc(steps, 1)
                pool.wait_ge(steps, g + 1)
                pool.tensor_tensor(ln.rs[:, :], ln.ve[:, :], half_m[0:ROWS, :], ALU.pow).then_inc(ready, 1)

            def r1(l, g, h, j):
                s = S[l.name]
                rstd(LNB, g, s.statsB, s.rstdB, s.poolR)

            def places(l, g, h, j):
                s = S[l.name]
                pool.wait_ge(s.scattered[h], 16 * TILES * TOP * j)
                past(pool, pool_passed)
                pool.tensor_copy(rows[h][:, :, :, PLACE].bitcast(I32), place[:, :, :]).then_inc(s.place_ready, 1)
                pool.wait_ge(s.place_ready, 2 * g + 1)
                past(pool, pool_passed)
                pool.tensor_scalar(place[:, :, :], place[:, :, :], float(TOP * GT), None, ALU.add)\
                    .then_inc(s.place_ready, 1)

            def send(l, g, h, first=0, end=TILES * TOP):
                s = S[l.name]
                pool.wait_ge(s.rows1_ready, g + 1)
                pool.wait_ge(s.gate_ready, g + 1)
                pool.wait_ge(s.slot_ready, g + 1)
                pool.wait_ge(s.place_ready, 2 * g + 2)
                past(pool, pool_passed)
                for n in range(first, end):
                    t, k = divmod(n, TOP)
                    pool.indirect_dma_start(
                        out=lists[l.name], out_offset=bass.IndirectOffsetOnAxis(ap=slots[h][:, t, k:k + 1], axis=0),
                        in_=rows[h][:, t, k, :], in_offset=None).then_inc(s.scattered[h], 16)

            def front_step(g, h, j, ahead):
                if ahead:
                    rstd(LNA, g + 1, statsA, rstdA, poolA)
                r1(L0, g, h, j)
                places(L0, g, h, j)
                if not (isinstance(g, int) and g == 0):
                    send(L0, g - 1, 1 - h)

            rstd(LNA, 0, statsA, rstdA, poolA)
            for h in range(2):
                front_step(h, h, 0, True)
            with pool.Fori(1, GROUPS // 2 - 1) as j:
                for h in range(2):
                    front_step(2 * j + h, h, j, True)
            j = GROUPS // 2 - 1
            front_step(2 * j, 0, j, True)
            front_step(2 * j + 1, 1, j, False)
            send(L0, GROUPS - 1, 1)

            def expert_blocks(l):
                k = K[l.name]
                def send_results(u, j):
                    pool.wait_ge(k.y_ready, k.i0 + l.unroll * j + u + 1)
                    past(pool, pool_passed)
                    for q in range(l.Q):
                        pool.indirect_dma_start(
                            out=results[l.name], out_offset=bass.IndirectOffsetOnAxis(
                                ap=xblk[u][:, q, PLACE:PLACE + 1].bitcast(U32), axis=0),
                            in_=yblk[u][:, q, :], in_offset=None, bounds_check=last, oob_is_err=False)\
                            .then_inc(k.y_out[u], 16)

                rounds(pool, l, send_results)

            expert_blocks(L0)

            def mid_a(g):
                rstd(LNA, g, m_statsA, m_rstdA, poolM)

            def mid_b(g):
                pool.wait_ge(ssq_ready, g + 1)
                pool.wait_ge(actx_ready, g)
                pool.tensor_tensor(mag[:, :], ssq[:, :], half_p[0:ROWS, :], ALU.pow).then_inc(mag_ready, 1)

            def mid_step(g, h, j, ahead, ahead2=True):
                sends = not (isinstance(g, int) and g == 0)
                r1(L1, g, h, j)
                places(L1, g, h, j)
                if sends:
                    send(L1, g - 1, 1 - h, 0, 4)
                if ahead2:
                    mid_a(g + 2)
                if sends:
                    send(L1, g - 1, 1 - h, 4, 5)
                if ahead:
                    mid_b(g + 1)
                if sends:
                    send(L1, g - 1, 1 - h, 5, TILES * TOP)

            for h in range(2):
                pool.wait_ge(S["L0"].scattered[h], 16 * TILES * TOP * GROUPS // 2)
            pool.tensor_copy(place[:, :, :], place0[:, :, :]).then_inc(made_step, 1)
            n[0] += 1
            pool.wait_ge(made_step, n[0])
            mid_a(0)
            mid_a(1)
            mid_b(0)
            for h in range(2):
                mid_step(h, h, 0, True)
            with pool.Fori(1, GROUPS // 2 - 1) as j:
                for h in range(2):
                    mid_step(2 * j + h, h, j, True)
            j = GROUPS // 2 - 1
            mid_step(2 * j, 0, j, True, False)
            mid_step(2 * j + 1, 1, j, False, False)
            send(L1, GROUPS - 1, 1)
            expert_blocks(L1)


def laid_out(v):
    import numpy as np
    f = {k: np.asarray(x) for k, x in v.items()}
    x = f["x"].reshape(GROUPS, GI, 3, 8, 28, 8, 28).transpose(0, 2, 4, 6, 1, 3, 5).reshape(GROUPS, IN_D, GP)
    main = x[:, :KT * 128].reshape(GROUPS, CHUNKS, KC, 128, GP).transpose(0, 1, 3, 2, 4)
    wT = f["L0_tok_W"].T
    w1 = f["L1_ffn_w1"].transpose(0, 2, 1)
    w2 = f["L1_ffn_w2"].transpose(0, 2, 1).reshape(L1.E, L1.FC, 128, D).transpose(0, 2, 1, 3)
    b1 = f["L1_ffn_b1"].reshape(L1.E, L1.FC, 128).transpose(0, 2, 1)
    b2 = np.broadcast_to(f["L1_ffn_b2"][:, None, :], (L1.E, 128, D))
    a = {
        "x_main": main.reshape(GROUPS * CHUNKS, 128, KC * GP),
        "x_rest": x[:, KT * 128:],
        "w_main": wT[:KT * 128].reshape(KT, 128, D).transpose(1, 0, 2).reshape(128, KT * D),
        "w_rest": wT[KT * 128:],
        "small": np.concatenate([
            f["L0_attn_Wq"], f["L0_attn_Wk"], f["L0_attn_Wv"], f["L0_tok_pos_embed"].T, f["L0_ffn_expert_sel"].T,
            f["L1_ffn_router_w"].T,
            np.stack([f["L0_tok_b"], f["L0_attn_bq"], f["L0_attn_bk"], f["L0_tok_class_token"][0]], 1)], 1),
        "per_row": np.concatenate([f["L0_attn_bv"], f["L1_ffn_router_b"], f["L1_attn_k"].reshape(1)])[None, :],
        "w_L0": np.concatenate([f["L0_ffn_keys"], f["L0_ffn_values"]], 2).reshape(L0.E * 128, L0.W),
        "w_L1": np.concatenate([w1, w2.reshape(L1.E, 128, L1.FC * D), b1, b2], 2).reshape(L1.E * 128, L1.W),
    }
    return {k: np.ascontiguousarray(x) for k, x in a.items()}


def kernel(**inputs):
    import concourse.bacc as bacc
    from concourse.bass_utils import run_bass_kernel_spmd
    arrays = laid_out(inputs)
    nc = bacc.Bacc("TRN2", target_bir_lowering=False, num_devices=1)
    a = {n: nc.dram_tensor(f"in_{n}", x.shape, mybir.dt.from_np(x.dtype), kind="ExternalInput").ap()
         for n, x in arrays.items()}
    out = nc.dram_tensor("out_0", (TOKENS, D), F32, kind="ExternalOutput").ap()
    build(nc, a, out)
    r = run_bass_kernel_spmd(nc, [{f"in_{n}": x for n, x in arrays.items()}], core_ids=[0])
    return r.results[0]["out_0"].reshape(IMAGES, SEQ, D)
```
